# Optimizing a Trainium2 kernel written in Bass

```python
import numpy as np
import jax
import jax.numpy as jnp

def _softmax(x, axis=-1):
    return jax.nn.softmax(x, axis=axis)

def _gelu(x):
    return jax.nn.gelu(x, approximate=True)

def _silu(x):
    return jax.nn.silu(x)

def _sigmoid(x):
    return jax.nn.sigmoid(x)

def _layernorm(x, axis=-1, eps=1e-05):
    m = jnp.mean(x, axis=axis, keepdims=True)
    v = jnp.var(x, axis=axis, keepdims=True)
    return (x - m) / jnp.sqrt(v + eps)

def _scatter_add(tgt, idx, src, axis=0):
    return tgt.at[idx].add(src)

def _segment_sum(src, seg, n):
    return jax.ops.segment_sum(src, seg, n)
kernel_name = 'mk_recurrent_d2_jaxref_r8_9d55b3'

def setup_inputs(seed: int=0):
    np.random.seed(seed)
    _w = jnp.asarray

    def _L0_attn_setup():
        import jax, jax.numpy as jnp
        import numpy as np

        def log_g(x):
            return jnp.where(x >= 0.0, jnp.log(jax.nn.relu(x) + 0.5), -jax.nn.softplus(-x))
        key = jax.random.key(seed)
        k1, k2 = jax.random.split(key)
        B, L, D = (4, 512, 128)
        x = jax.random.normal(k1, (B, L, D), dtype=jnp.float32)
        W = jax.random.normal(k2, (2 * D, D), dtype=jnp.float32) * (1.0 / np.sqrt(D))
        return {'x': x, 'W': W}
    _L0_attn_in = _L0_attn_setup()

    def _L0_ffn_setup():
        import jax, jax.numpy as jnp
        import numpy as np
        DIM, HEADS, EXPERTS, DFF = (128, 16, 8, 512)
        EPS = 1e-05

        def layernorm(x, g, b):
            mu = jnp.mean(x, -1, keepdims=True)
            var = jnp.mean(jnp.square(x - mu), -1, keepdims=True)
            return (x - mu) * jax.lax.rsqrt(var + EPS) * g + b
        key = jax.random.key(seed)
        ks = jax.random.split(key, 12)
        s = lambda d: 1.0 / np.sqrt(d)
        return {'x': jax.random.normal(ks[0], (2, 256, DIM), jnp.float32), 'conv_w': jax.random.normal(ks[1], (DIM, DIM, 3), jnp.float32) * s(DIM * 3), 'conv_b': jnp.zeros((DIM,), jnp.float32), 'wqkv': jax.random.normal(ks[2], (3 * DIM, DIM), jnp.float32) * s(DIM), 'bqkv': jnp.zeros((3 * DIM,), jnp.float32), 'wo': jax.random.normal(ks[3], (DIM, DIM), jnp.float32) * s(DIM), 'bo': jnp.zeros((DIM,), jnp.float32), 'ln1_g': jnp.ones((DIM,), jnp.float32), 'ln1_b': jnp.zeros((DIM,), jnp.float32), 'gate_w': jax.random.normal(ks[4], (DIM, EXPERTS), jnp.float32) * s(DIM), 'gate_b': jnp.zeros((EXPERTS,), jnp.float32), 'w1': jax.random.normal(ks[5], (EXPERTS, DIM, DFF), jnp.float32) * s(DIM), 'b1': jnp.zeros((EXPERTS, DFF), jnp.float32), 'w2': jax.random.normal(ks[6], (EXPERTS, DFF, DIM), jnp.float32) * s(DFF), 'b2': jnp.zeros((EXPERTS, DIM), jnp.float32), 'ln2_g': jnp.ones((DIM,), jnp.float32), 'ln2_b': jnp.zeros((DIM,), jnp.float32)}
    _L0_ffn_in = _L0_ffn_setup()

    def _L1_attn_setup():
        import jax, jax.numpy as jnp
        import numpy as np
        B, K, D = (8, 256, 128)
        INNER = 2 * D
        EPS = 1e-05

        def _silu(x):
            return x * jax.nn.sigmoid(x)
        key = jax.random.key(seed)
        k0, k1, k2, k3 = jax.random.split(key, 4)
        s_in = 1.0 / np.sqrt(D)
        s_inner = 1.0 / np.sqrt(INNER)
        return {'x': jax.random.normal(k0, (B, K, D), dtype=jnp.float32), 'w_norm': jnp.ones((D,), dtype=jnp.float32), 'W_in': (jax.random.normal(k1, (2 * INNER, D)) * s_in).astype(jnp.float32), 'W_dt': (jax.random.normal(k2, (INNER, INNER)) * s_inner).astype(jnp.float32), 'b_dt': jnp.zeros((INNER,), dtype=jnp.float32), 'W_out': (jax.random.normal(k3, (D, INNER)) * s_inner).astype(jnp.float32)}
    _L1_attn_in = _L1_attn_setup()

    def _L1_ffn_setup():
        import jax, jax.numpy as jnp
        import numpy as np
        B, N, D, F, E, K = (4, 256, 128, 512, 16, 2)
        EPS = 1e-05
        key = jax.random.key(seed)
        ks = jax.random.split(key, 6)
        scaled = lambda k, shape, fan: jax.random.normal(k, shape, jnp.float32) / np.float32(np.sqrt(fan))
        return {'x': jax.random.normal(ks[0], (B, N, D), jnp.float32), 'Wr': scaled(ks[1], (D, E), D), 'br': jnp.zeros((E,), jnp.float32), 'W1': scaled(ks[2], (E, D, F), D), 'W3': scaled(ks[3], (E, D, F), D), 'W2': scaled(ks[4], (E, F, D), F), 'gamma': jnp.ones((E, D), jnp.float32), 'beta': jnp.zeros((E, D), jnp.float32)}
    _L1_ffn_in = _L1_ffn_setup()
    _d = {'L0_attn_x': _L0_attn_in['x'], 'L0_attn_W': _L0_attn_in['W'], 'L0_ffn_conv_w': _L0_ffn_in['conv_w'], 'L0_ffn_conv_b': _L0_ffn_in['conv_b'], 'L0_ffn_wqkv': _L0_ffn_in['wqkv'], 'L0_ffn_bqkv': _L0_ffn_in['bqkv'], 'L0_ffn_wo': _L0_ffn_in['wo'], 'L0_ffn_bo': _L0_ffn_in['bo'], 'L0_ffn_ln1_g': _L0_ffn_in['ln1_g'], 'L0_ffn_ln1_b': _L0_ffn_in['ln1_b'], 'L0_ffn_gate_w': _L0_ffn_in['gate_w'], 'L0_ffn_gate_b': _L0_ffn_in['gate_b'], 'L0_ffn_w1': _L0_ffn_in['w1'], 'L0_ffn_b1': _L0_ffn_in['b1'], 'L0_ffn_w2': _L0_ffn_in['w2'], 'L0_ffn_b2': _L0_ffn_in['b2'], 'L0_ffn_ln2_g': _L0_ffn_in['ln2_g'], 'L0_ffn_ln2_b': _L0_ffn_in['ln2_b'], 'L1_attn_w_norm': _L1_attn_in['w_norm'], 'L1_attn_W_in': _L1_attn_in['W_in'], 'L1_attn_W_dt': _L1_attn_in['W_dt'], 'L1_attn_b_dt': _L1_attn_in['b_dt'], 'L1_attn_W_out': _L1_attn_in['W_out'], 'L1_ffn_Wr': _L1_ffn_in['Wr'], 'L1_ffn_br': _L1_ffn_in['br'], 'L1_ffn_W1': _L1_ffn_in['W1'], 'L1_ffn_W3': _L1_ffn_in['W3'], 'L1_ffn_W2': _L1_ffn_in['W2'], 'L1_ffn_gamma': _L1_ffn_in['gamma'], 'L1_ffn_beta': _L1_ffn_in['beta']}
    _x0 = _d['L0_attn_x']
    _d['L0_attn_x'] = jax.random.normal(jax.random.fold_in(jax.random.key(seed), 1), (1, 2048, 128), dtype=_x0.dtype)
    del _x0
    return _d

def reference(L0_attn_x, L0_attn_W, L0_ffn_conv_w, L0_ffn_conv_b, L0_ffn_wqkv, L0_ffn_bqkv, L0_ffn_wo, L0_ffn_bo, L0_ffn_ln1_g, L0_ffn_ln1_b, L0_ffn_gate_w, L0_ffn_gate_b, L0_ffn_w1, L0_ffn_b1, L0_ffn_w2, L0_ffn_b2, L0_ffn_ln2_g, L0_ffn_ln2_b, L1_attn_w_norm, L1_attn_W_in, L1_attn_W_dt, L1_attn_b_dt, L1_attn_W_out, L1_ffn_Wr, L1_ffn_br, L1_ffn_W1, L1_ffn_W3, L1_ffn_W2, L1_ffn_gamma, L1_ffn_beta):

    def _L0_attn_ref(x, W):
        import jax, jax.numpy as jnp
        import numpy as np

        def log_g(x):
            return jnp.where(x >= 0.0, jnp.log(jax.nn.relu(x) + 0.5), -jax.nn.softplus(-x))
        D = x.shape[-1]
        hg = jnp.einsum('bld,ed->ble', x, W)
        hidden, gate = (hg[..., :D], hg[..., D:])
        log_coeffs = -jax.nn.softplus(gate)
        log_z = -jax.nn.softplus(-gate)
        log_tilde_h = log_g(hidden)
        log_values = log_z + log_tilde_h
        a_star = jnp.cumsum(log_coeffs, axis=1)
        log_h0_plus_b_star = jax.lax.cumlogsumexp(log_values - a_star, axis=1)
        log_h = a_star + log_h0_plus_b_star
        return jnp.exp(log_h)

    def _L0_ffn_ref(x, conv_w, conv_b, wqkv, bqkv, wo, bo, ln1_g, ln1_b, gate_w, gate_b, w1, b1, w2, b2, ln2_g, ln2_b):
        import jax, jax.numpy as jnp
        import numpy as np
        DIM, HEADS, EXPERTS, DFF = (128, 16, 8, 512)
        EPS = 1e-05

        def layernorm(x, g, b):
            mu = jnp.mean(x, -1, keepdims=True)
            var = jnp.mean(jnp.square(x - mu), -1, keepdims=True)
            return (x - mu) * jax.lax.rsqrt(var + EPS) * g + b
        B, S, D = x.shape
        H, dh = (HEADS, D // HEADS)
        xt = jnp.transpose(x, (0, 2, 1))
        xt = jax.lax.conv_general_dilated(xt, conv_w, (1,), [(1, 1)], dimension_numbers=('NCH', 'OIH', 'NCH'))
        x = jnp.transpose(xt + conv_b[None, :, None], (0, 2, 1))
        qkv = x @ wqkv.T + bqkv
        q, k, v = jnp.split(qkv, 3, axis=-1)
        q = q.reshape(B, S, H, dh).transpose(0, 2, 1, 3)
        k = k.reshape(B, S, H, dh).transpose(0, 2, 1, 3)
        v = v.reshape(B, S, H, dh).transpose(0, 2, 1, 3)
        scores = jnp.einsum('bhqd,bhkd->bhqk', q, k) / jnp.sqrt(jnp.float32(dh))
        attn = jax.nn.softmax(scores, axis=-1)
        ctx = jnp.einsum('bhqk,bhkd->bhqd', attn, v)
        ctx = ctx.transpose(0, 2, 1, 3).reshape(B, S, D)
        attn_out = ctx @ wo.T + bo
        x = layernorm(x + attn_out, ln1_g, ln1_b)
        probs = jax.nn.softmax(x @ gate_w + gate_b, axis=-1)
        h = jax.nn.relu(jnp.einsum('bsd,edf->bsef', x, w1) + b1)
        y = jnp.einsum('bsef,efd->bsed', h, w2) + b2
        moe_out = jnp.einsum('bse,bsed->bsd', probs, y)
        x = layernorm(x + moe_out, ln2_g, ln2_b)
        return x

    def _L1_attn_ref(x, w_norm, W_in, W_dt, b_dt, W_out):
        import jax, jax.numpy as jnp
        import numpy as np
        B, K, D = (8, 256, 128)
        INNER = 2 * D
        EPS = 1e-05

        def _silu(x):
            return x * jax.nn.sigmoid(x)
        h = x * jax.lax.rsqrt(jnp.mean(x * x, axis=-1, keepdims=True) + EPS) * w_norm
        uv = jnp.einsum('bkd,ed->bke', h, W_in)
        u, z = (uv[..., :INNER], uv[..., INNER:])
        u = _silu(u)
        lam = jax.nn.sigmoid(jnp.einsum('bki,ji->bkj', u, W_dt) + b_dt)

        def step(s, inp):
            lam_t, u_t = inp
            s = lam_t * s + (1.0 - lam_t) * u_t
            return (s, s)
        lam_k = jnp.moveaxis(lam, 1, 0)
        u_k = jnp.moveaxis(u, 1, 0)
        s0 = jnp.zeros((x.shape[0], INNER), dtype=x.dtype)
        _, ys = jax.lax.scan(step, s0, (lam_k, u_k))
        s = jnp.moveaxis(ys, 0, 1)
        s = s * _silu(z)
        y = jnp.einsum('bki,di->bkd', s, W_out)
        return x + y

    def _L1_ffn_ref(x, Wr, br, W1, W3, W2, gamma, beta):
        import jax, jax.numpy as jnp
        import numpy as np
        B, N, D, F, E, K = (4, 256, 128, 512, 16, 2)
        EPS = 1e-05
        b, n, d = x.shape
        e = Wr.shape[1]
        xf = x.reshape(-1, d)
        logits = xf @ Wr + br
        probs = jax.nn.softmax(logits, axis=-1)
        vals, idx = jax.lax.top_k(probs, K)
        w = vals / vals.sum(axis=-1, keepdims=True)
        combine = jnp.zeros((xf.shape[0], e), x.dtype)
        for k in range(K):
            combine = combine + w[:, k:k + 1] * jax.nn.one_hot(idx[:, k], e, dtype=x.dtype)
        out = jnp.zeros_like(xf)
        for ei in range(e):
            h = jax.nn.silu(xf @ W1[ei]) * (xf @ W3[ei])
            y = h @ W2[ei]
            mu = y.mean(axis=-1, keepdims=True)
            var = ((y - mu) ** 2).mean(axis=-1, keepdims=True)
            y = (y - mu) * jax.lax.rsqrt(var + EPS) * gamma[ei] + beta[ei]
            out = out + combine[:, ei:ei + 1] * y
        return out.reshape(b, n, d)
    x = L0_attn_x
    xn = _layernorm(x, axis=-1)
    s = _L0_attn_ref(xn, L0_attn_W)
    g = _silu(_L0_ffn_ref(xn, L0_ffn_conv_w, L0_ffn_conv_b, L0_ffn_wqkv, L0_ffn_bqkv, L0_ffn_wo, L0_ffn_bo, L0_ffn_ln1_g, L0_ffn_ln1_b, L0_ffn_gate_w, L0_ffn_gate_b, L0_ffn_w1, L0_ffn_b1, L0_ffn_w2, L0_ffn_b2, L0_ffn_ln2_g, L0_ffn_ln2_b))
    x = x + s * g
    xn = _layernorm(x, axis=-1)
    s = _L1_attn_ref(xn, L1_attn_w_norm, L1_attn_W_in, L1_attn_W_dt, L1_attn_b_dt, L1_attn_W_out)
    g = _silu(_L1_ffn_ref(xn, L1_ffn_Wr, L1_ffn_br, L1_ffn_W1, L1_ffn_W3, L1_ffn_W2, L1_ffn_gamma, L1_ffn_beta))
    x = x + s * g
    return x

_drawn_inputs = setup_inputs


def setup_inputs(seed=0):
    import zlib

    import numpy as np

    out = dict(_drawn_inputs(seed))
    spreads = {'L0_ffn_conv_b': (0.0, 0.1),
     'L0_ffn_bqkv': (0.0, 0.1),
     'L0_ffn_bo': (0.0, 0.1),
     'L0_ffn_ln1_g': (1.0, 0.2),
     'L0_ffn_ln1_b': (0.0, 0.1),
     'L0_ffn_gate_b': (0.0, 0.1),
     'L0_ffn_b1': (0.0, 0.1),
     'L0_ffn_b2': (0.0, 0.1),
     'L0_ffn_ln2_g': (1.0, 0.2),
     'L0_ffn_ln2_b': (0.0, 0.1),
     'L1_attn_w_norm': (1.0, 0.558),
     'L1_attn_b_dt': (0.0, 0.8),
     'L1_ffn_br': (0.0, 0.1),
     'L1_ffn_gamma': (1.0, 0.2),
     'L1_ffn_beta': (0.0, 0.1)}
    factors = {}
    for name, (base, spread) in spreads.items():
        noise = np.random.default_rng([zlib.crc32(name.encode()), seed]).standard_normal(out[name].shape)
        drawn = base * np.exp(spread * noise) if base else spread * noise
        out[name] = jnp.asarray(drawn.astype(out[name].dtype))
    for name, factor in factors.items():
        out[name] = (out[name] * factor).astype(out[name].dtype)
    return out
```

```python
from contextlib import ExitStack

import concourse.bass as bass
from concourse import mybir

ALU = mybir.AluOpType
ACT = mybir.ActivationFunctionType
AX = mybir.AxisListType
F32 = mybir.dt.float32
BF16 = mybir.dt.bfloat16
U32 = mybir.dt.uint32

P = 128
N = 2048
T = N // P
CH = 512
C = N // CH
TC = CH // P
EPS = 1e-5

H = 16
DH = P // H
PARTS = 3
STACK = PARTS * PARTS * DH
MROW = 96
KS = MROW + PARTS
RING = 4
VW = 32

E0, F0 = 8, 512
E1, F1 = 16, 512
FT = F0 // P
LOOP = 8
NT = LOOP * -(-((2 * N + (P - 1) * E1) // P) // LOOP)
INNER = 2 * P

MATS = {}
_at = 0
for _name, _w in (("gru", 2 * P), ("conv", 3 * P), ("qkv", 3 * P), ("ident", P),
                  ("wo", P), ("gate", E0), ("wr", E1), ("win", 2 * INNER), ("wdt", 2 * INNER),
                  ("wout", 2 * P)):
    MATS[_name] = (_at, _at + _w)
    _at += _w
MATS_W = _at
MATS_1 = MATS["ident"][1]
COLS = {}
_at = 0
for _name, _w in (("conv_b", 1), ("bq", 1), ("bk", 1), ("b1", E0 * FT), ("b_dt", 2), ("w_norm", 1)):
    COLS[_name] = (_at, _at + _w)
    _at += _w
COLS_W = _at
ROWS = {}
_at = 0
for _name, _w in (("bv", P), ("bo", P), ("ln1_g", P), ("ln1_b", P), ("ln2_g", P), ("ln2_b", P),
                  ("gate_b", E0), ("br", E1), ("iota", NT), ("gamma", E1 * P), ("beta", E1 * P)):
    ROWS[_name] = (_at, _at + _w)
    _at += _w
ROWS_W = _at
W_ALL = 3 * F1
PICK = 32


class Chain:

    def __init__(self, eng, sem):
        self.eng, self.sem, self.base, self.n = eng, sem, 0, 0

    def did(self, ins):
        ins.then_inc(self.sem, 1)
        self.n += 1

    def settle(self):
        self.eng.wait_ge(self.sem, self.base + self.n)

    def step(self, ins):
        self.did(ins)
        self.settle()

    def total(self):
        return self.base + self.n

    def at(self, count):
        self.base, self.n = count, 0


class Steps:

    def __init__(self, **steps):
        self.banks, self.before, at = steps, {}, 0
        for name, n in steps.items():
            self.before[name] = at
            at += n
        self.total = at

    def n(self, step, c=None):
        return self.before[step] + (self.banks[step] if c is None else c + 1)


def bank_of(n):
    return (n - 1) % 8


def build(nc, x, mats, cols, rows, b2, pick, tri, w1, w2, w_all, out):
    with ExitStack() as ctx:
        def sb(name, shape, dt=F32):
            return ctx.enter_context(nc.sbuf_tensor(name, shape, dt))

        def sem(name):
            return ctx.enter_context(nc.semaphore(name))

        x_sb = sb("x_sb", [P, T, P])
        xn = sb("xn", [P, T, P])
        xnT = sb("xnT", [P, N + 2])
        sT = sb("sT", [P, N])
        xcT = sb("xcT", [P, N])
        big = sb("big", [P, E1 * W_ALL])
        qf = big[:, 0:N]
        kf = big[:, N:2 * N]
        qparts = big[:, 2 * N:4 * N - N // 2].bitcast(BF16).rearrange("p (a n) -> p a n", a=PARTS)
        kparts = big[:, 4 * N - N // 2:5 * N].bitcast(BF16).rearrange("p (a n) -> p a n", a=PARTS)
        q_ring = big[:, 5 * N:7 * N].bitcast(BF16)
        k_ring = big[:, 7 * N:9 * N].bitcast(BF16)
        probs_f = big[:, 9 * N:11 * N]
        probs = probs_f.rearrange("p (s q) -> p s q", s=8)
        V = big[:, 11 * N:12 * N].rearrange("p (t d) -> p t d", t=T)
        Vo = sb("Vo", [P, T * VW + CH])
        Vh = Vo[:, 0:T * VW].rearrange("p (t w) -> p t w", t=T)
        o_sum = Vo[:, T * VW:T * VW + CH]
        tmpT = sb("tmpT", [P, N])
        ctx_sb = sb("ctx_sb", [P, T, P])
        mat_sb = sb("mat_sb", [P, MATS_W])
        col_sb = sb("col_sb", [P, COLS_W])
        row_sb = sb("row_sb", [P, ROWS_W])
        b2_sb = sb("b2_sb", [E0, P])
        pick_sb = sb("pick_sb", [PARTS * PICK, E0 * P], BF16)
        w1_buf = sb("w1_buf", [P, 2, F0])
        w2_buf = sb("w2_buf", [P, 2, F0])
        ident_bf = sb("ident_bf", [P, P], BF16)
        stats = sb("stats", [P, T, 6])
        moments = sb("moments", [P, T, 2])
        rstd = sb("rstd", [P, T])
        mx = sb("mx", [P, 2, 8])
        neg_m = sb("neg_m", [P, TC])
        m_rest = sb("m_rest", [P, TC])
        m_parts = sb("m_parts", [P, PARTS, TC], BF16)
        zeros = sb("zeros", [P, TC])
        mT = sb("mT", [PARTS * TC, P], BF16)
        o_inv = sb("o_inv", [P, T])
        sig_h, gate_z, gate_c = probs_f[:, 0:N], probs_f[:, N:2 * N], tmpT
        ctxT = tmpT
        x1 = xn
        x1T = xnT[:, 0:N]
        gate_p = sb("gate_p", [P, T, E0])
        gate_rest = sb("gate_rest", [P, T, E0])
        gate_s = sb("gate_s", [P, T])
        gate_parts = sb("gate_parts", [P, T, PARTS * PICK], BF16)
        p_stack = xcT[0:PARTS * PICK, 0:N // 2].bitcast(BF16)
        h_relu = xcT[:, N // 2:N].rearrange("p (s q) -> p s q", s=2)
        h_wt = ctx_sb[:, :, :].rearrange("p t d -> p (t d)").rearrange("p (s q) -> p s q", s=4)
        pT = tmpT[0:E0, :]
        xn2 = xn
        xn2T = tmpT
        hN = ctx_sb
        hT = xnT[:, 0:N]
        u = [sT, xcT]
        lam = [tmpT, ctx_sb[:, :, :].rearrange("p t d -> p (t d)")]
        z_tmp = [w1_buf[:, 0, :], w1_buf[:, 1, :], w2_buf[:, 0, :], w2_buf[:, 1, :]]
        s1 = sT[:, :].rearrange("p (t d) -> p t d", t=T)
        y1 = xcT[:, :].rearrange("p (t d) -> p t d", t=T)
        y2 = tmpT[:, :].rearrange("p (t d) -> p t d", t=T)
        tri_bf = sb("tri_bf", [P, 2 * P], BF16)
        rms = sb("rms", [P, T])
        route = w1_buf[:, :, :].rearrange("p a f -> p (a f)")
        rp, place = (route[:, i * T * E1:(i + 1) * T * E1].rearrange("p (t e) -> p t e", t=T) for i in range(2))
        tot, upto = (route[:, i * T * E1:(i + 1) * T * E1].rearrange("p (e t) -> p e t", t=T) for i in range(2, 4))
        rs = sb("rs", [P, T])
        top = sb("top", [P, T, 8])
        top_i = sb("top_i", [P, T, 8], U32)
        top_f = sb("top_f", [P, 2, T])
        wgt = sb("wgt", [P, 2, T])
        hot = w2_buf[:, 0, :].rearrange("p (k t e) -> p k t e", k=2, t=T)
        mask = sb("mask", [P, T, E1], BF16)
        reset = sb("reset", [P, E1, T])
        n_tiles = sb("n_tiles", [P, E1])
        end = sb("end", [P, E1])
        pos = sb("pos", [P, 2, T])
        pos_i = sb("pos_i", [P, 2, T], U32)
        te_thr = sb("te_thr", [P, T])
        te = sb("te", [1, NT])
        te_i = sb("te_i", [1, NT], U32)
        te_cmp = hN[0:1, 0:NT * E1 // P, :].rearrange("p a b -> p (a b)").rearrange("p (t e) -> p t e", e=E1)
        xt = w1_buf[:, 0, :].rearrange("p (s d) -> p s d", s=4)
        xtT = w1_buf[:, 1, :].rearrange("p (s d) -> p s d", s=4)
        hid = Vo[:, 0:2 * CH].rearrange("p (s f) -> p s f", s=2)
        hidT = w2_buf
        y_ring = xnT[:, 0:LOOP * P].rearrange("p (s d) -> p s d", s=LOOP)
        y_mom = sb("y_mom", [P, LOOP, 2])
        y_st = sb("y_st", [P, LOOP, 6])
        y_rstd = sb("y_rstd", [P, LOOP])
        xg_dram = nc.dram_tensor("xg_dram", [NT * P, P], F32, kind="Internal").ap()
        yg_dram = nc.dram_tensor("yg_dram", [NT * P, P], F32, kind="Internal").ap()
        PS = ctx.enter_context(nc.psum_tensor("PS", [P, 8, CH], F32))
        parts_dram = nc.dram_tensor("parts_dram", [2, PARTS, P, N], BF16, kind="Internal").ap()

        def mat(name):
            return mat_sb[:, MATS[name][0]:MATS[name][1]]

        def col(name, i=0):
            return col_sb[:, COLS[name][0] + i:COLS[name][0] + i + 1]

        def row(name):
            return row_sb[:, ROWS[name][0]:ROWS[name][1]]

        ident = mat("ident")

        x_in = [sem(f"x_in{c}") for c in range(C)]
        mats_in = sem("mats_in")
        mats2_in = sem("mats2_in")
        cols_in = sem("cols_in")
        rows_in = sem("rows_in")
        consts_set = sem("consts_set")
        act_chain = sem("act_chain")
        dve_chain = sem("dve_chain")
        pool_chain = sem("pool_chain")
        ln_var = sem("ln_var")
        ln_std = sem("ln_std")
        xn_ready = sem("xn_ready")
        pa_mm = sem("pa_mm")
        pa_act = sem("pa_act")
        pa_dve = sem("pa_dve")
        gru_sig = sem("gru_sig")
        split_q = sem("split_q")
        split_k = sem("split_k")
        parts_out = sem("parts_out")
        heads_in = sem("heads_in")
        s_ready = sem("s_ready")
        exp_done = sem("exp_done")
        mx_ready = sem("mx_ready")
        mx_used = sem("mx_used")
        mx_chunk = sem("mx_chunk")
        mp_ready = sem("mp_ready")
        mt_ready = sem("mt_ready")
        mt_copied = sem("mt_copied")
        m_rows = sem("m_rows")
        v_ready = sem("v_ready")
        pv_done = sem("pv_done")
        o_copied = sem("o_copied")
        ot_ready = sem("ot_ready")
        o_used = sem("o_used")
        out_done = sem("out_done")
        head0_in = sem("head0_in")
        small_in = sem("small_in")
        w1_in = [sem("w1_in0"), sem("w1_in1")]
        w2_in = [sem("w2_in0"), sem("w2_in1")]
        c_mm = sem("c_mm")
        c_act = sem("c_act")
        c_dve = sem("c_dve")
        bias_seen = sem("bias_seen")
        ln1_done = sem("ln1_done")
        probs_exp = sem("probs_exp")
        pp_ready = sem("pp_ready")
        h_mm = sem("h_mm")
        h_act = sem("h_act")
        h_dve = sem("h_dve")
        p_mm = sem("p_mm")
        y_mm = sem("y_mm")
        r_dve = sem("r_dve")
        wall_in = sem("wall_in")
        zero_out = sem("zero_out")
        norm3 = sem("norm3")
        rms_sum = sem("rms_sum")
        rms_root = sem("rms_root")
        h_norm = sem("h_norm")
        route_exp = sem("route_exp")
        mask_set = sem("mask_set")
        pos_set = sem("pos_set")
        te_set = sem("te_set")
        scattered = sem("scattered")
        d_mm = sem("d_mm")
        d_act = sem("d_act")
        d_dve = sem("d_dve")
        u_gated = sem("u_gated")
        z_used = sem("z_used")
        s_gated = sem("s_gated")
        xt_in = [sem(f"xt_in{i}") for i in range(4)]
        xt_mm = sem("xt_mm")
        xt_act = sem("xt_act")
        g_mm = sem("g_mm")
        g_act = sem("g_act")
        g_dve = sem("g_dve")
        gt_mm = sem("gt_mm")
        gt_act = sem("gt_act")
        yt_mm = sem("yt_mm")
        yt_dve = sem("yt_dve")
        y_var = sem("y_var")
        y_std = sem("y_std")
        y_norm = sem("y_norm")
        y_out = sem("y_out")
        y1_in = sem("y1_in")
        mixed = sem("mixed")
        silu1 = sem("silu1")
        done = sem("done")
        e_mm = sem("e_mm")
        e_act = sem("e_act")
        e_dve = sem("e_dve")
        norm2 = sem("norm2")
        silu0 = sem("silu0")
        x_ready = sem("x_ready")
        identb_set = sem("identb_set")

        block = ctx.enter_context(nc.Block())

        PA_MM = Steps(T=C, X=C, Q=C, K=C, V=C, GD=2 * C)
        PA_ACT = Steps(T=C, X=C, GD=2 * C)
        PA_DVE = Steps(Q=C, K=C, V=C)
        C_MM = Steps(U=C, O=C, Y=C, G=1, p=C, s=2)
        C_ACT = Steps(U=C, Y=C, p=C, s=2)
        C_DVE = Steps(O=C, G=1)
        HB, PB = 4, 6
        E_MM = Steps(R=C, S=C)
        D_MM = Steps(A=C, L=1, B=C, U=2 * C, K=1, M=2 * C, Z=2 * C, Y=C)
        D_ACT = Steps(A=C, B=C, U=2 * C, M=2 * C, Z=2 * C)
        D_DVE = Steps(L=1, K=1, Y=C)
        H1B, H3B, GB, XB, YB = 0, 2, 4, 5, 6
        SB, MB, PVB, MISC = 0, 2, 6, 7

        def d_free(eng):
            eng.wait_ge(z_used, 2 * C)

        @block.sync
        def _(sp):
            xv = x.rearrange("(t p) d -> p t d", p=P)
            for c in range(C):
                sp.dma_start(x_sb[:, c * TC:(c + 1) * TC, :], xv[:, c * TC:(c + 1) * TC, :]).then_inc(x_in[c], 16)
            for who, parts, ready in ((0, qparts, split_q), (1, kparts, split_k)):
                for p in range(PARTS):
                    sp.wait_ge(ready, p + 1)
                    sp.dma_start(parts_dram[who, p], parts[:, p, :]).then_inc(parts_out, 16)

            def load_head(h, landed):
                at = bass.ds((h % RING) * N, N)
                for a in range(PARTS):
                    rows_a = slice(a * PARTS * DH, (a + 1) * PARTS * DH)
                    sp.dma_start(q_ring[rows_a, at],
                                 parts_dram[0, a, bass.ds(h * DH, DH), :].partition_broadcast(PARTS))\
                        .then_inc(landed, 16)
                    sp.dma_start(k_ring[rows_a, at],
                                 parts_dram[1, :, bass.ds(h * DH, DH), :]).then_inc(landed, 16)

            def place_maxima(m):
                sp.wait_ge(mt_copied, m + 1)
                at = (m // C % RING) * N + (m % C) * CH
                sp.dma_start(q_ring[MROW:KS, bass.ds(at, CH)], mT[:, :]).then_inc(m_rows, 16)

            sp.wait_ge(parts_out, 16 * 2 * PARTS)
            sp.wait_ge(consts_set, 1)
            load_head(0, head0_in)
            load_head(1, heads_in)
            load_head(2, heads_in)
            for m in range(C):
                place_maxima(m)
            sp.wait_ge(heads_in, 96 * 2)
            load_head(3, heads_in)
            for m in range(C, 2 * C):
                place_maxima(m)
            with sp.Fori(1, H - RING + 1) as h:
                sp.wait_ge(pv_done, h * T)
                sp.wait_ge(heads_in, 96 * (h + 2))
                load_head(h + RING - 1, heads_in)
                with sp.Fori(0, C) as c:
                    place_maxima(C * (h + 1) + c)
            with sp.Fori(C * (H - RING + 2), C * H) as m:
                place_maxima(m)
            sp.wait_ge(o_used, H)
            sp.wait_ge(c_mm, 1)
            for k in range(4):
                w = E1 * W_ALL // 4
                sp.dma_start(big[:, k * w:(k + 1) * w], w_all[:, k * w:(k + 1) * w]).then_inc(wall_in, 16)
            for e in range(2, E0, 2):
                for par in range(2):
                    sp.wait_ge(h_mm, C * FT * (e + par - 1))
                    sp.dma_start(w1_buf[:, par, :], w1[e + par]).then_inc(w1_in[par], 16)
                    sp.wait_ge(y_mm, C * FT * (e + par - 1))
                    sp.dma_start(w2_buf[:, par, :], w2[e + par]).then_inc(w2_in[par], 16)
            sp.wait_ge(scattered, 16 * 2 * T)

            def load_tile(n, k):
                sp.dma_start(xt[:, k, :], xg_dram[bass.ds(n * P, P), :]).then_inc(xt_in[k], 16)

            def store_tiles(b, half):
                sp.wait_ge(y_norm, b + 1)
                sp.dma_start(yg_dram[bass.ds(b * 4 * P, 4 * P), :].rearrange("(t p) d -> p t d", p=P),
                             y_ring[:, 4 * half:4 * half + 4, :]).then_inc(y_out, 16)

            d_free(sp)
            for k in range(4):
                load_tile(k, k)
            for k in range(4):
                sp.wait_ge(xt_mm, k + 1)
                load_tile(4 + k, k)
            with sp.Fori(1, NT // LOOP) as b:
                for half in range(2):
                    for k in range(4):
                        n = LOOP * b + 4 * half + k
                        sp.wait_ge(xt_mm, n - 3)
                        load_tile(n, k)
                    store_tiles(2 * b - 2 + half, half)
            for half in range(2):
                store_tiles(NT // 4 - 2 + half, half)
            xo = out.rearrange("(t p) d -> p t d", p=P)
            for c in range(C):
                sp.wait_ge(done, c + 1)
                sp.dma_start(xo[:, c * TC:(c + 1) * TC, :], x_sb[:, c * TC:(c + 1) * TC, :]).then_inc(out_done, 16)
            sp.wait_ge(out_done, 16 * C)

        @block.gpsimd
        def _(pool):
            ch = Chain(pool, pool_chain)
            ch.step(nc.gpsimd.memset(xnT[:, 0:1], 0.0))
            ch.step(nc.gpsimd.memset(xnT[:, N + 1:N + 2], 0.0))
            ch.step(nc.gpsimd.memset(q_ring[64:MROW, :].bitcast(F32), 0.0))
            ch.step(nc.gpsimd.memset(k_ring[64:MROW, :].bitcast(F32), 0.0))
            ch.step(nc.gpsimd.memset(k_ring[MROW:KS, :], 1.0))
            nc.gpsimd.memset(zeros[:, :], 0.0).then_inc(consts_set, 1)
            pool.wait_ge(consts_set, 1)
            ch.step(nc.gpsimd.memset(Vh[:, :, :], 0.0))
            ch.step(nc.gpsimd.memset(Vh[:, :, DH:DH + 1], 1.0))
            nc.gpsimd.memset(gate_parts[:, :, :], 0.0).then_inc(consts_set, 1)
            pool.wait_ge(consts_set, 2)
            ch.step(nc.gpsimd.memset(reset[:, :, :], 1.0))
            ch.step(nc.gpsimd.memset(reset[:, :, 0:1], 0.0))
            ch.step(nc.gpsimd.memset(ctx_sb[:, :, :], 0.0))
            for k in range(NT // T):
                pool.dma_start(xg_dram.rearrange("(p n) d -> p (n d)", p=P)[:, k * N:(k + 1) * N],
                               ctx_sb[:, :, :].rearrange("p t d -> p (t d)")).then_inc(zero_out, 16)

            def copy_values(h):
                pool.wait_ge(consts_set, 1)
                nc.gpsimd.tensor_copy(Vh[:, :, 0:DH], V[:, :, bass.ds(h * DH, DH)]).then_inc(v_ready, 1)

            def split_maxima(m):
                pool.wait_ge(mx_chunk, m + 1)
                ch.step(nc.gpsimd.tensor_tensor(m_parts[:, 0, :], neg_m[:, :], zeros[:, :], ALU.add))
                ch.step(nc.gpsimd.tensor_tensor(m_rest[:, :], neg_m[:, :], m_parts[:, 0, :], ALU.subtract))
                ch.step(nc.gpsimd.tensor_tensor(m_parts[:, 1, :], m_rest[:, :], zeros[:, :], ALU.add))
                ch.step(nc.gpsimd.tensor_tensor(m_rest[:, :], m_rest[:, :], m_parts[:, 1, :], ALU.subtract))
                nc.gpsimd.tensor_tensor(m_parts[:, 2, :], m_rest[:, :], zeros[:, :], ALU.add).then_inc(mp_ready, 1)

            pool.wait_ge(pa_dve, PA_DVE.n("V"))
            copy_values(0)
            split_maxima(0)
            start = ch.total() - 4
            with pool.Fori(1, C) as m:
                ch.at(start + 4 * m)
                pool.wait_ge(mt_ready, m)
                split_maxima(m)
            with pool.Fori(0, H - 1) as h:
                with pool.Fori(0, C) as c:
                    m = C * (h + 1) + c
                    ch.at(start + 4 * m)
                    pool.wait_ge(mt_ready, m)
                    split_maxima(m)
                pool.wait_ge(pv_done, (h + 1) * T)
                copy_values(h + 1)

            pool.wait_ge(zero_out, 16 * (NT // T))
            pool.wait_ge(pos_set, 1)
            for t in range(T):
                for k in range(2):
                    pool.indirect_dma_start(xg_dram[:, :], bass.IndirectOffsetOnAxis(ap=pos_i[:, k, t:t + 1], axis=0),
                                            xn2[:, t, :], None).then_inc(scattered, 16)
            d_free(pool)
            pool.wait_ge(s_gated, C)
            pool.wait_ge(y_out, 16 * (NT // 4))
            for t in range(T):
                for k, y in enumerate((y1, y2)):
                    pool.indirect_dma_start(y[:, t, :], None, yg_dram[:, :],
                                            bass.IndirectOffsetOnAxis(ap=pos_i[:, k, t:t + 1], axis=0))\
                        .then_inc(y1_in, 16)

        @block.scalar
        def _(act):
            act.dma_start(mat_sb[:, 0:MATS_1], mats[:, 0:MATS_1]).then_inc(mats_in, 16)
            act.dma_start(col_sb[:, :], cols[:, :]).then_inc(cols_in, 16)
            act.dma_start(row_sb[:, :], rows.partition_broadcast(P)).then_inc(rows_in, 16)
            act.dma_start(mat_sb[:, MATS_1:MATS_W], mats[:, MATS_1:MATS_W]).then_inc(mats2_in, 16)
            act.dma_start(b2_sb[:, :], b2[:, :]).then_inc(small_in, 16)
            act.dma_start(pick_sb[:, :], pick[:, :]).then_inc(small_in, 16)
            act.dma_start(tri_bf[:, :], tri[:, :]).then_inc(small_in, 16)
            for par in range(2):
                act.dma_start(w1_buf[:, par, :], w1[par]).then_inc(w1_in[par], 16)
                act.dma_start(w2_buf[:, par, :], w2[par]).then_inc(w2_in[par], 16)
            for c in range(C):
                act.wait_ge(ln_var, c + 1)
                nc.scalar.activation(rstd[:, c * TC:(c + 1) * TC], rstd[:, c * TC:(c + 1) * TC], ACT.Sqrt)\
                    .then_inc(ln_std, 1)
            act.wait_ge(mats_in, 16)
            nc.scalar.copy(ident_bf[:, :], ident).then_inc(identb_set, 1)
            for c in range(C):
                n = PA_MM.n("T", c)
                act.wait_ge(pa_mm, n)
                nc.scalar.copy(xnT[:, 1 + c * CH:1 + (c + 1) * CH], PS[:, bank_of(n), :]).then_inc(pa_act, 1)
            act.wait_ge(cols_in, 16)
            for c in range(C):
                n = PA_MM.n("X", c)
                act.wait_ge(pa_mm, n)
                nc.scalar.activation(xcT[:, c * CH:(c + 1) * CH], PS[:, bank_of(n), :], ACT.Identity,
                                     bias=col("conv_b")).then_inc(pa_act, 1)
            for c in range(C):
                at = slice(c * CH, (c + 1) * CH)
                n = PA_MM.n("GD", 2 * c)
                act.wait_ge(pa_mm, n)
                nc.scalar.activation(sT[:, at], PS[:, bank_of(n), :], ACT.Relu).then_inc(gru_sig, 1)
                nc.scalar.activation(sig_h[:, at], PS[:, bank_of(n), :], ACT.Sigmoid).then_inc(pa_act, 1)
                n = PA_MM.n("GD", 2 * c + 1)
                act.wait_ge(pa_mm, n)
                nc.scalar.activation(gate_z[:, at], PS[:, bank_of(n), :], ACT.Sigmoid).then_inc(gru_sig, 1)
                nc.scalar.activation(gate_c[:, at], PS[:, bank_of(n), :], ACT.Sigmoid, scale=-1.0).then_inc(pa_act, 1)

            def copy_maxima(m):
                act.wait_ge(mt_ready, m + 1)
                if not (isinstance(m, int) and m == 0):
                    act.wait_ge(m_rows, 16 * m)
                nc.scalar.copy(mT[:, :], PS[0:PARTS * TC, MISC, 0:P // 2].bitcast(BF16)).then_inc(mt_copied, 1)

            def exps(h, k):
                if not (isinstance(h, int) and h == 0 and k < 2):
                    act.wait_ge(pv_done, h * T + k - 1)
                for i in range(C):
                    act.wait_ge(s_ready, (h * T + k) * C + i + 1)
                    nc.scalar.activation(probs[:, C * (k % 2) + i, :], PS[:, SB + i % 2, :], ACT.Exp,
                                         scale=DH ** -0.5).then_inc(exp_done, 1)

            def copy_output(h):
                act.wait_ge(pv_done, (h + 1) * T)
                if not (isinstance(h, int) and h == 0):
                    act.wait_ge(ot_ready, h)
                nc.scalar.copy(o_sum[:, :], PS[:, PVB, :]).then_inc(o_copied, 1)

            def head(h, output, maxima):
                for k in range(T):
                    exps(h, k)
                    if k == 0 and output:
                        copy_output(h - 1)
                    if k % 4 == 2 and maxima:
                        copy_maxima(C * (h + 1) + k // 4)

            for m in range(C):
                copy_maxima(m)
            head(0, False, True)
            with act.Fori(1, H - 1) as h:
                head(h, True, True)
            head(H - 1, True, False)
            copy_output(H - 1)

            for c in range(C):
                act.wait_ge(c_mm, C_MM.n("U", c))
                nc.scalar.copy(ctxT[:, c * CH:(c + 1) * CH], PS[:, bank_of(C_MM.n("U", c)), :]).then_inc(c_act, 1)
            for c in range(C):
                act.wait_ge(ln_var, C + c + 1)
                nc.scalar.activation(rstd[:, c * TC:(c + 1) * TC], rstd[:, c * TC:(c + 1) * TC], ACT.Sqrt)\
                    .then_inc(ln_std, 1)
            for c in range(C):
                act.wait_ge(c_mm, C_MM.n("Y", c))
                nc.scalar.copy(x1T[:, c * CH:(c + 1) * CH], PS[:, bank_of(C_MM.n("Y", c)), :]).then_inc(c_act, 1)
            act.wait_ge(probs_exp, 1)
            nc.scalar.activation(gate_p[:, :, :], gate_p[:, :, :], ACT.Exp).then_inc(probs_exp, 1)
            for c in range(C):
                act.wait_ge(c_mm, C_MM.n("p", c))
                nc.scalar.copy(pT[:, c * CH:(c + 1) * CH], PS[0:E0, bank_of(C_MM.n("p", c)), :]).then_inc(c_act, 1)
            for c in range(2):
                act.wait_ge(c_mm, C_MM.n("s", c))
                nc.scalar.copy(p_stack[:, c * 2 * CH:(c + 1) * 2 * CH],
                               PS[0:PARTS * PICK, bank_of(C_MM.n("s", c)), :].bitcast(BF16)).then_inc(c_act, 1)

            def rectify(e, c, f):
                unit = (e * C + c) * FT + f
                act.wait_ge(h_mm, unit + 1)
                if not (isinstance(e, int) and unit < 2):
                    act.wait_ge(h_dve, unit - 1)
                act.nop().then_inc(bias_seen, 1)
                nc.scalar.activation(h_relu[:, f % 2, :], PS[:, HB + f % 2, :], ACT.Relu,
                                     bias=col_sb[:, bass.ds(COLS["b1"][0] + e * FT + f, 1)]).then_inc(h_act, 1)

            for c in range(C):
                for f in range(FT):
                    rectify(0, c, f)
            with act.Fori(1, E0) as e:
                for c in range(C):
                    for f in range(FT):
                        rectify(e, c, f)
            act.wait_ge(bias_seen, E0 * C * FT)
            for c in range(C):
                act.wait_ge(e_mm, E_MM.n("R", c))
                nc.scalar.copy(x1[:, c * TC:(c + 1) * TC, :].rearrange("p t d -> p (t d)"),
                               PS[:, bank_of(E_MM.n("R", c) + C), :]).then_inc(e_act, 1)
            for c in range(C):
                act.wait_ge(ln_var, 2 * C + c + 1)
                nc.scalar.activation(rstd[:, c * TC:(c + 1) * TC], rstd[:, c * TC:(c + 1) * TC], ACT.Sqrt)\
                    .then_inc(ln_std, 1)
            for c in range(C):
                act.wait_ge(norm2, c + 1)
                nc.scalar.activation(x1[:, c * TC:(c + 1) * TC, :], x1[:, c * TC:(c + 1) * TC, :], ACT.Silu)\
                    .then_inc(silu0, 1)

            for c in range(C):
                at = slice(c * TC, (c + 1) * TC)
                act.wait_ge(ln_var, 3 * C + c + 1)
                nc.scalar.activation(rstd[:, at], rstd[:, at], ACT.Sqrt).then_inc(ln_std, 1)
            for c in range(C):
                at = slice(c * TC, (c + 1) * TC)
                act.wait_ge(rms_sum, c + 1)
                nc.scalar.activation(rms[:, at], rms[:, at], ACT.Sqrt).then_inc(rms_root, 1)
            for c in range(C):
                act.wait_ge(d_mm, D_MM.n("A", c))
                nc.scalar.copy(xn2T[:, c * CH:(c + 1) * CH], PS[:, bank_of(D_MM.n("A", c)), :]).then_inc(d_act, 1)
            act.wait_ge(route_exp, 1)
            nc.scalar.activation(rp[:, :, :], rp[:, :, :], ACT.Exp).then_inc(route_exp, 1)
            for c in range(C):
                act.wait_ge(d_mm, D_MM.n("B", c))
                nc.scalar.activation(hT[:, c * CH:(c + 1) * CH], PS[:, bank_of(D_MM.n("B", c)), :], ACT.Copy,
                                     scale=col("w_norm")).then_inc(d_act, 1)
            for j in range(2):
                for c in range(C):
                    n = D_MM.n("U", j * C + c)
                    act.wait_ge(d_mm, n)
                    nc.scalar.activation(u[j][:, c * CH:(c + 1) * CH], PS[:, bank_of(n), :], ACT.Silu)\
                        .then_inc(d_act, 1)
            for j in range(2):
                for c in range(C):
                    n = D_MM.n("M", j * C + c)
                    act.wait_ge(d_mm, n)
                    if j:
                        act.wait_ge(te_set, 1)
                    nc.scalar.activation(lam[j][:, c * CH:(c + 1) * CH], PS[:, bank_of(n), :], ACT.Sigmoid,
                                         bias=col("b_dt", j)).then_inc(d_act, 1)
            act.wait_ge(pos_set, 1)
            for j in range(2):
                for c in range(C):
                    n = D_MM.n("Z", j * C + c)
                    act.wait_ge(d_mm, n)
                    if j:
                        act.wait_ge(z_used, c + 1)
                    nc.scalar.activation(z_tmp[c], PS[:, bank_of(n), :], ACT.Silu).then_inc(d_act, 1)

            def copy_slots(n, k):
                act.wait_ge(xt_mm, n + 1)
                if not (isinstance(n, int) and n < 4):
                    act.wait_ge(g_mm, n - 3)
                nc.scalar.copy(xtT[:, k % 4, :], PS[:, XB, 0:P]).then_inc(xt_act, 1)

            def gate_slots(n, k):
                act.wait_ge(g_mm, n + 1)
                if not (isinstance(n, int) and n < 2):
                    act.wait_ge(gt_mm, n - 1)
                nc.scalar.activation(hid[:, k % 2, :], PS[:, H1B + k % 2, :], ACT.Silu).then_inc(g_act, 1)

            def copy_hidden(n, k):
                act.wait_ge(gt_mm, n + 1)
                if not (isinstance(n, int) and n < 2):
                    act.wait_ge(yt_mm, n - 1)
                nc.scalar.copy(hidT[:, k % 2, :], PS[:, GB, :]).then_inc(gt_act, 1)

            def roots(b, half):
                act.wait_ge(y_var, b + 1)
                at = slice(4 * half, 4 * half + 4)
                nc.scalar.activation(y_rstd[:, at], y_rstd[:, at], ACT.Sqrt).then_inc(y_std, 1)

            def experts_act(b, first, last):
                for k in range(LOOP):
                    n = LOOP * b + k
                    if not (last and k == LOOP - 1):
                        gate_slots(n + 1, k + 1)
                    copy_hidden(n, k)
                    if not (last and k >= LOOP - 2):
                        copy_slots(n + 2, k + 2)
                    if k == 1 and not first:
                        roots(2 * b - 1, 1)
                    if k == 5:
                        roots(2 * b, 0)

            d_free(act)
            copy_slots(0, 0)
            copy_slots(1, 1)
            gate_slots(0, 0)
            experts_act(0, True, False)
            with act.Fori(1, NT // LOOP - 1) as b:
                experts_act(b, False, False)
            experts_act(NT // LOOP - 1, False, True)
            roots(NT // 4 - 1, 1)
            for c in range(C):
                act.wait_ge(mixed, c + 1)
                nc.scalar.activation(y1[:, c * TC:(c + 1) * TC, :], y1[:, c * TC:(c + 1) * TC, :], ACT.Silu)\
                    .then_inc(silu1, 1)

        @block.vector
        def _(dve):
            ch = Chain(dve, dve_chain)
            v = nc.vector

            for c in range(C):
                dve.wait_ge(x_in[c], 16)
                for t in range(c * TC, (c + 1) * TC):
                    ch.did(v.bn_stats(stats[:, t, :], x_sb[:, t, :]))
                ch.settle()
                for t in range(c * TC, (c + 1) * TC):
                    ch.did(v.bn_aggr(moments[:, t, :], stats[:, t, :]))
                ch.settle()
                v.tensor_scalar(rstd[:, c * TC:(c + 1) * TC], moments[:, c * TC:(c + 1) * TC, 1], EPS, None,
                                ALU.add).then_inc(ln_var, 1)
            for c in range(C):
                dve.wait_ge(ln_std, c + 1)
                ch.step(v.reciprocal(rstd[:, c * TC:(c + 1) * TC], rstd[:, c * TC:(c + 1) * TC]))
                for t in range(c * TC, (c + 1) * TC):
                    v.tensor_scalar(xn[:, t, :], x_sb[:, t, :], moments[:, t, 0:1], rstd[:, t:t + 1],
                                    ALU.subtract, ALU.mult).then_inc(xn_ready, 1)

            dve.wait_ge(cols_in, 16)
            dve.wait_ge(rows_in, 16)
            for kind, full, parts, bias, ready in (("Q", qf, qparts, "bq", split_q), ("K", kf, kparts, "bk", split_k)):
                for c in range(C):
                    n = PA_MM.n(kind, c)
                    dve.wait_ge(pa_mm, n)
                    v.tensor_scalar(full[:, c * CH:(c + 1) * CH], PS[:, bank_of(n), :], col(bias), None, ALU.add)\
                        .then_inc(pa_dve, 1)
                dve.wait_ge(pa_dve, PA_DVE.n(kind))
                for p in range(PARTS):
                    v.tensor_copy(parts[:, p, :], full[:, :]).then_inc(ready, 1)
                    if p < PARTS - 1:
                        dve.wait_ge(ready, p + 1)
                        ch.step(v.tensor_tensor(full[:, :], full[:, :], parts[:, p, :], ALU.subtract))
            for c in range(C):
                n = PA_MM.n("V", c)
                dve.wait_ge(pa_mm, n)
                v.tensor_tensor(V[:, c * TC:(c + 1) * TC, :],
                                PS[:, bank_of(n), :].rearrange("p (t d) -> p t d", t=TC),
                                row("bv").unsqueeze(1).broadcast_to([P, TC, P]), ALU.add).then_inc(pa_dve, 1)
            for c in range(C):
                at = slice(c * CH, (c + 1) * CH)
                dve.wait_ge(gru_sig, 2 * (c + 1))
                dve.wait_ge(pa_act, PA_ACT.n("GD", 2 * c))
                ch.step(v.scalar_tensor_tensor(sT[:, at], sig_h[:, at], 0.5, sT[:, at], ALU.min, ALU.add))
                ch.step(v.tensor_tensor(sT[:, at], sT[:, at], gate_z[:, at], ALU.mult))
            dve.wait_ge(pa_act, PA_ACT.total)
            ch.did(v.tensor_tensor_scan(sT[:, :], gate_c[:, :], sT[:, :], 0.0, ALU.mult, ALU.add))

            def maxima(m, c, upto=TC, since=0):
                for j in range(since, upto):
                    if j == 0 and not (isinstance(m, int) and m < 2):
                        dve.wait_ge(mx_chunk, m - 1)
                    for half in range(2):
                        dve.wait_ge(mx_ready, 8 * m + 2 * j + half + 1)
                        v.tensor_reduce(mx[:, c % 2, 2 * j + half:2 * j + half + 1],
                                        PS[:, MB + 2 * half:MB + 2 * half + 2, :].rearrange("p b n -> p (b n)"),
                                        AX.X, ALU.max).then_inc(mx_used, 1)
                if upto == TC:
                    dve.wait_ge(mx_used, 8 * (m + 1))
                    if not (isinstance(m, int) and m == 0):
                        dve.wait_ge(mp_ready, m)
                    v.tensor_reduce(neg_m[:, :], mx[:, c % 2, :].rearrange("p (t b) -> p t b", b=2),
                                    AX.X, ALU.max, negate=True).then_inc(mx_chunk, 1)

            def normalise(h):
                dve.wait_ge(ot_ready, h + 1)
                o = PS[:, MISC, :].rearrange("p (i c w) -> p i c w", i=TC, c=C)
                inv = o_inv[:, :].rearrange("p (i c) -> p i c", i=TC)
                ch.step(v.reciprocal(inv, o[:, :, :, DH]))
                v.tensor_tensor(ctx_sb[:, :, bass.ds(h * DH, DH)].rearrange("p (c i) d -> p i c d", c=C),
                                o[:, :, :, 0:DH], inv.unsqueeze(3).broadcast_to([P, TC, C, DH]),
                                ALU.mult).then_inc(o_used, 1)

            for m in range(C + 1):
                maxima(m, m % C)
            dve.wait_ge(zero_out, 16 * (NT // T))
            for c in range(C):
                maxima(C + 1 + c, (c + 1) % C)
            start = ch.total() - 1
            with dve.Fori(1, H - 2) as h:
                ch.at(start + h)
                m = C * h + C + 1
                maxima(m, 1)
                maxima(m + 1, 2, upto=2)
                normalise(h - 1)
                maxima(m + 1, 2, since=2)
                maxima(m + 2, 3)
                maxima(m + 3, 0)
            ch.at(start + H - 2)
            m = C * (H - 1) + 1
            maxima(m, 1)
            maxima(m + 1, 2, upto=2)
            normalise(H - 3)
            maxima(m + 1, 2, since=2)
            maxima(m + 2, 3)
            normalise(H - 2)
            normalise(H - 1)

            def chunk(buf, c):
                return buf[:, c * TC:(c + 1) * TC, :]

            def bc(name, k=P):
                return row(name).unsqueeze(1).broadcast_to([P, TC, k])

            def norm_stats(buf, c):
                for t in range(c * TC, (c + 1) * TC):
                    ch.did(v.bn_stats(stats[:, t, :], buf[:, t, :]))
                ch.settle()
                for t in range(c * TC, (c + 1) * TC):
                    ch.did(v.bn_aggr(moments[:, t, :], stats[:, t, :]))
                ch.settle()
                v.tensor_scalar(rstd[:, c * TC:(c + 1) * TC], moments[:, c * TC:(c + 1) * TC, 1], EPS, None,
                                ALU.add).then_inc(ln_var, 1)

            def norm_apply(buf, c, gain, shift, done, calls):
                dve.wait_ge(ln_std, C * calls + c + 1)
                ch.step(v.reciprocal(rstd[:, c * TC:(c + 1) * TC], rstd[:, c * TC:(c + 1) * TC]))
                for t in range(c * TC, (c + 1) * TC):
                    ch.did(v.tensor_scalar(buf[:, t, :], buf[:, t, :], moments[:, t, 0:1], rstd[:, t:t + 1],
                                           ALU.subtract, ALU.mult))
                ch.settle()
                ch.step(v.tensor_tensor(chunk(buf, c), chunk(buf, c), bc(gain), ALU.mult))
                v.tensor_tensor(chunk(buf, c), chunk(buf, c), bc(shift), ALU.add).then_inc(done, 1)

            for c in range(C):
                n = C_MM.n("O", c)
                dve.wait_ge(c_mm, n)
                v.tensor_tensor(chunk(x1, c), PS[:, bank_of(n), :].rearrange("p (t d) -> p t d", t=TC),
                                bc("bo"), ALU.add).then_inc(c_dve, 1)
                dve.wait_ge(c_dve, C_DVE.n("O", c))
                norm_stats(x1, c)
            for c in range(C):
                norm_apply(x1, c, "ln1_g", "ln1_b", ln1_done, 1)
            dve.wait_ge(c_mm, C_MM.n("G"))
            v.tensor_tensor(gate_p[:, :, :], PS[:, bank_of(C_MM.n("G")), 0:T * E0].rearrange("p (t e) -> p t e", e=E0),
                            row("gate_b").unsqueeze(1).broadcast_to([P, T, E0]), ALU.add).then_inc(c_dve, 1)
            dve.wait_ge(c_dve, C_DVE.n("G"))
            ch.step(v.tensor_reduce(gate_s[:, :], gate_p[:, :, :], AX.X, ALU.max))
            v.tensor_tensor(gate_p[:, :, :], gate_p[:, :, :], gate_s[:, :].unsqueeze(2).broadcast_to([P, T, E0]),
                            ALU.subtract).then_inc(probs_exp, 1)
            dve.wait_ge(probs_exp, 2)
            ch.step(v.tensor_reduce(gate_s[:, :], gate_p[:, :, :], AX.X, ALU.add))
            ch.step(v.reciprocal(gate_s[:, :], gate_s[:, :]))
            v.tensor_tensor(gate_p[:, :, :], gate_p[:, :, :], gate_s[:, :].unsqueeze(2).broadcast_to([P, T, E0]),
                            ALU.mult).then_inc(pp_ready, 1)
            dve.wait_ge(pp_ready, 1)
            dve.wait_ge(consts_set, 2)
            for p in range(PARTS):
                part = gate_parts[:, :, p * PICK:p * PICK + E0]
                rest = gate_p if p == 0 else gate_rest
                ch.step(v.tensor_copy(part, rest[:, :, :]))
                if p < PARTS - 1:
                    ch.step(v.tensor_tensor(gate_rest[:, :, :], rest[:, :, :], part, ALU.subtract))
            dve.nop().then_inc(pp_ready, 1)

            def weigh(e, c, f):
                unit = (e * C + c) * FT + f
                if f == 0:
                    dve.wait_ge(p_mm, e * C + c + 1)
                dve.wait_ge(h_act, unit + 1)
                if not (isinstance(e, int) and unit < 4):
                    dve.wait_ge(y_mm, unit - 3)
                v.tensor_tensor(h_wt[:, f, :], h_relu[:, f % 2, :], PS[:, PB + c % 2, :], ALU.mult)\
                    .then_inc(h_dve, 1)

            for c in range(C):
                for f in range(FT):
                    weigh(0, c, f)
            with dve.Fori(1, E0) as e:
                for c in range(C):
                    for f in range(FT):
                        weigh(e, c, f)
            for c in range(C):
                dve.wait_ge(y_mm, E0 * C * FT)
                v.tensor_tensor(ctxT[:, c * CH:(c + 1) * CH], PS[:, c, :], x1T[:, c * CH:(c + 1) * CH], ALU.add)\
                    .then_inc(r_dve, 1)
            for c in range(C):
                dve.wait_ge(e_act, c + 1)
                norm_stats(x1, c)
            for c in range(C):
                norm_apply(x1, c, "ln2_g", "ln2_b", norm2, 2)
            for c in range(C):
                dve.wait_ge(silu0, c + 1)
                dve.wait_ge(e_mm, E_MM.n("S", c))
                v.tensor_tensor(chunk(x1, c), chunk(x1, c),
                                PS[:, bank_of(E_MM.n("S", c) + C), :].rearrange("p (t d) -> p t d", t=TC),
                                ALU.mult).then_inc(e_dve, 1)
                dve.wait_ge(e_dve, c + 1)
                v.tensor_tensor(chunk(x_sb, c), chunk(x_sb, c), chunk(x1, c), ALU.add).then_inc(x_ready, 1)

            for c in range(C):
                dve.wait_ge(x_ready, c + 1)
                norm_stats(x_sb, c)
            for c in range(C):
                dve.wait_ge(ln_std, C * 3 + c + 1)
                ch.step(v.reciprocal(rstd[:, c * TC:(c + 1) * TC], rstd[:, c * TC:(c + 1) * TC]))
                for t in range(c * TC, (c + 1) * TC):
                    v.tensor_scalar(xn2[:, t, :], x_sb[:, t, :], moments[:, t, 0:1], rstd[:, t:t + 1],
                                    ALU.subtract, ALU.mult).then_inc(norm3, 1)
                dve.wait_ge(norm3, (c + 1) * TC)
                for t in range(c * TC, (c + 1) * TC):
                    ch.did(v.tensor_tensor_reduce(hN[:, t, :], xn2[:, t, :], xn2[:, t, :], 1.0 / P, 0.0,
                                                  ALU.mult, ALU.add, rms[:, t:t + 1]))
                ch.settle()
                v.tensor_scalar(rms[:, c * TC:(c + 1) * TC], rms[:, c * TC:(c + 1) * TC], EPS, None, ALU.add)\
                    .then_inc(rms_sum, 1)
            for c in range(C):
                dve.wait_ge(rms_root, c + 1)
                ch.step(v.reciprocal(rms[:, c * TC:(c + 1) * TC], rms[:, c * TC:(c + 1) * TC]))
                for t in range(c * TC, (c + 1) * TC):
                    v.tensor_scalar(hN[:, t, :], xn2[:, t, :], rms[:, t:t + 1], None, ALU.mult).then_inc(h_norm, 1)

            def over_e(a):
                return a.unsqueeze(2).broadcast_to([P, T, E1])

            dve.wait_ge(d_mm, D_MM.n("L"))
            v.tensor_tensor(rp[:, :, :], PS[:, bank_of(D_MM.n("L")), 0:T * E1].rearrange("p (t e) -> p t e", e=E1),
                            row("br").unsqueeze(1).broadcast_to([P, T, E1]), ALU.add).then_inc(d_dve, 1)
            dve.wait_ge(d_dve, D_DVE.n("L"))
            ch.step(v.tensor_reduce(rs[:, :], rp[:, :, :], AX.X, ALU.max))
            v.tensor_tensor(rp[:, :, :], rp[:, :, :], over_e(rs[:, :]), ALU.subtract).then_inc(route_exp, 1)
            dve.wait_ge(route_exp, 2)
            ch.step(v.tensor_reduce(rs[:, :], rp[:, :, :], AX.X, ALU.add))
            ch.step(v.reciprocal(rs[:, :], rs[:, :]))
            ch.step(v.tensor_tensor(rp[:, :, :], rp[:, :, :], over_e(rs[:, :]), ALU.mult))
            for t in range(T):
                ch.did(v.max(top[:, t, :], rp[:, t, :]))
            ch.settle()
            for t in range(T):
                ch.did(v.max_index(top_i[:, t, :], top[:, t, :], rp[:, t, :]))
            ch.did(v.tensor_tensor(rs[:, :], top[:, :, 0], top[:, :, 1], ALU.add))
            ch.settle()
            ch.did(v.tensor_copy(top_f[:, :, :], top_i[:, :, 0:2].rearrange("p t k -> p k t")))
            ch.did(v.reciprocal(rs[:, :], rs[:, :]))
            ch.settle()
            for k in range(2):
                ch.did(v.tensor_tensor(wgt[:, k, :], top[:, :, k], rs[:, :], ALU.mult))
                ch.did(v.tensor_tensor(hot[:, k, :, :], row("iota")[:, 0:E1].unsqueeze(1).broadcast_to([P, T, E1]),
                                       over_e(top_f[:, k, :]), ALU.is_equal))
            ch.settle()
            v.tensor_tensor(mask[:, :, :], hot[:, 0, :, :], hot[:, 1, :, :], ALU.add).then_inc(mask_set, 1)

            n = D_MM.n("K")
            dve.wait_ge(d_mm, n)
            kb = PS[:, bank_of(n), :].rearrange("p (a t e) -> p a t e", a=2, t=T)
            ch.step(v.tensor_copy(tot[:, :, :], kb[:, 1, :, :].rearrange("p t e -> p e t")))
            ch.step(v.tensor_tensor_scan(upto[:, :, :].rearrange("p e t -> p (e t)"),
                                         reset[:, :, :].rearrange("p e t -> p (e t)"),
                                         tot[:, :, :].rearrange("p e t -> p (e t)"), 0.0, ALU.mult, ALU.add))
            ch.step(v.tensor_scalar(te_thr[:, :], row("iota")[:, 0:T], float(P), None, ALU.mult))
            ch.step(v.tensor_tensor(place[:, :, :].rearrange("p t e -> p (t e)").rearrange("p (e t) -> p e t", e=E1),
                                    upto[:, :, T - 1:T].broadcast_to([P, E1, T]),
                                    te_thr[:, :].unsqueeze(1).broadcast_to([P, E1, T]), ALU.is_gt))
            ch.step(v.tensor_reduce(n_tiles[:, :], place[:, :, :].rearrange("p t e -> p (t e)").rearrange("p (e t) -> p e t", e=E1), AX.X, ALU.add))
            ch.step(v.tensor_tensor_scan(end[:, :], reset[:, 0, 1:2].broadcast_to([P, E1]), n_tiles[:, :], 0.0,
                                         ALU.mult, ALU.add))
            ch.step(v.tensor_tensor(upto[:, :, :], upto[:, :, :], tot[:, :, :], ALU.subtract))
            ch.step(v.tensor_tensor(n_tiles[:, :], end[:, :], n_tiles[:, :], ALU.subtract))
            ch.step(v.scalar_tensor_tensor(upto[:, :, :], n_tiles[:, :].unsqueeze(2).broadcast_to([P, E1, T]), float(P),
                                           upto[:, :, :], ALU.mult, ALU.add))
            v.tensor_tensor(place[:, :, :], upto[:, :, :].rearrange("p e t -> p t e"), kb[:, 0, :, :],
                            ALU.add).then_inc(d_dve, 1)
            dve.wait_ge(d_dve, D_DVE.n("K"))
            for k in range(2):
                ch.step(v.tensor_tensor(hot[:, k, :, :], hot[:, k, :, :], place[:, :, :], ALU.mult))
                ch.step(v.tensor_reduce(pos[:, k, :], hot[:, k, :, :], AX.X, ALU.add))
            v.tensor_copy(pos_i[:, :, :], pos[:, :, :]).then_inc(pos_set, 1)
            dve.wait_ge(d_act, D_ACT.n("B"))
            dve.wait_ge(d_mm, D_MM.n("B"))
            ch.step(v.tensor_tensor(te_cmp, row("iota")[0:1, :].unsqueeze(2).broadcast_to([1, NT, E1]),
                                    end[0:1, :].unsqueeze(1).broadcast_to([1, NT, E1]), ALU.is_ge))
            ch.step(v.tensor_reduce(te[:, :], te_cmp, AX.X, ALU.add))
            v.tensor_scalar(te_i[:, :], te[:, :], float(E1 - 1), None, ALU.min).then_inc(te_set, 1)

            dve.wait_ge(d_act, D_ACT.n("M"))
            for j in range(2):
                ch.step(v.scalar_tensor_tensor(u[j][:, :], lam[j][:, :], 1.0, u[j][:, :], ALU.subtract, ALU.mult))
                ch.step(v.tensor_tensor_scan(lam[j][:, :], lam[j][:, :], u[j][:, :], 0.0, ALU.mult, ALU.subtract))
            for j in range(2):
                for c in range(C):
                    dve.wait_ge(d_act, D_ACT.n("Z", j * C + c))
                    v.tensor_tensor(lam[j][:, c * CH:(c + 1) * CH], lam[j][:, c * CH:(c + 1) * CH], z_tmp[c],
                                    ALU.mult).then_inc(z_used, 1)
            for c in range(C):
                n = D_MM.n("Y", c)
                dve.wait_ge(d_mm, n)
                v.tensor_tensor(chunk(s1, c), PS[:, bank_of(n), :].rearrange("p (t d) -> p t d", t=TC),
                                chunk(xn2, c), ALU.add).then_inc(d_dve, 1)
            dve.wait_ge(d_dve, D_DVE.n("Y"))
            dve.nop().then_inc(s_gated, C)

            def multiply(n, k):
                dve.wait_ge(g_act, n + 1)
                v.tensor_tensor(hid[:, k % 2, :], hid[:, k % 2, :], PS[:, H3B + k % 2, :], ALU.mult).then_inc(g_dve, 1)

            def take_output(n, k):
                dve.wait_ge(yt_mm, n + 1)
                if k % 4 == 0 and not (isinstance(n, int) and n < LOOP):
                    dve.wait_ge(y_out, 4 * n - 16)
                v.tensor_copy(y_ring[:, k, :], PS[:, YB + k % 2, 0:P]).then_inc(yt_dve, 1)
                dve.wait_ge(yt_dve, n + 1)
                ch.step(v.bn_stats(y_st[:, k, :], y_ring[:, k, :]))
                ch.did(dve.nop())
                ch.step(v.bn_aggr(y_mom[:, k, :], y_st[:, k, :]))
                if k % 4 == 3:
                    v.tensor_scalar(y_rstd[:, k - 3:k + 1], y_mom[:, k - 3:k + 1, 1], EPS, None, ALU.add)                        .then_inc(y_var, 1)

            def finish_outputs(b, half):
                dve.wait_ge(y_std, b + 1)
                at = slice(4 * half, 4 * half + 4)
                ch.step(v.reciprocal(y_rstd[:, at], y_rstd[:, at]))
                for k in range(4 * half, 4 * half + 4):
                    e = dve.value_load(te_i[0:1, bass.ds(4 * b + k % 4, 1)], min_val=0, max_val=E1 - 1)
                    ch.step(v.tensor_scalar(y_ring[:, k, :], y_ring[:, k, :], y_mom[:, k, 0:1], y_rstd[:, k:k + 1],
                                            ALU.subtract, ALU.mult))
                    ch.step(v.tensor_tensor(y_ring[:, k, :], y_ring[:, k, :], row("gamma")[:, bass.ds(e * P, P)], ALU.mult))
                    ch.step(v.tensor_tensor(y_ring[:, k, :], y_ring[:, k, :], row("beta")[:, bass.ds(e * P, P)], ALU.add))
                dve.nop().then_inc(y_norm, 1)

            def experts_dve(b, first, last):
                for k in range(LOOP):
                    n = LOOP * b + k
                    if not (last and k == LOOP - 1):
                        multiply(n + 1, k + 1)
                    if not (first and k == 0):
                        take_output(n - 1, (k - 1) % LOOP)
                    if k == 2 and not first:
                        finish_outputs(2 * b - 1, 1)
                    if k == 6:
                        finish_outputs(2 * b, 0)

            dve.wait_ge(te_set, 1)
            multiply(0, 0)
            experts_dve(0, True, False)
            per = LOOP * 3 + 2 * (1 + 12)
            start = ch.total()
            with dve.Fori(1, NT // LOOP - 1) as b:
                ch.at(start + (b - 1) * per)
                experts_dve(b, False, False)
                assert ch.n == per, ch.n
            ch.at(start + (NT // LOOP - 2) * per)
            experts_dve(NT // LOOP - 1, False, True)
            take_output(NT - 1, LOOP - 1)
            finish_outputs(NT // 4 - 1, 1)

            for c in range(C):
                dve.wait_ge(y1_in, 16 * 2 * T)
                for t in range(c * TC, (c + 1) * TC):
                    ch.did(v.tensor_scalar(y1[:, t, :], y1[:, t, :], wgt[:, 0, t:t + 1], None, ALU.mult))
                ch.settle()
                for t in range(c * TC, (c + 1) * TC):
                    ch.did(v.scalar_tensor_tensor(y1[:, t, :], y2[:, t, :], wgt[:, 1, t:t + 1], y1[:, t, :],
                                                  ALU.mult, ALU.add))
                ch.settle()
                dve.nop().then_inc(mixed, 1)
            for c in range(C):
                dve.wait_ge(silu1, c + 1)
                ch.step(v.tensor_tensor(chunk(y1, c), chunk(y1, c), chunk(s1, c), ALU.mult))
                v.tensor_tensor(chunk(x_sb, c), chunk(x_sb, c), chunk(y1, c), ALU.add).then_inc(done, 1)

        @block.tensor
        def _(pe):
            pe.wait_ge(mats_in, 16)

            def transposes(c):
                def mms(bank):
                    for i in range(TC):
                        pe.wait_ge(xn_ready, c * TC + i + 1)
                        last = pe.transpose(bank[:, i * P:(i + 1) * P], xn[:, c * TC + i, :], ident)
                    return last
                return mms

            def conv(c):
                def mms(bank):
                    pe.wait_ge(pa_act, min(c + 2, C))
                    for k in range(3):
                        last = pe.matmul(bank, mat("conv")[:, k * P:(k + 1) * P], xnT[:, c * CH + k:c * CH + k + CH],
                                         start=(k == 0), stop=(k == 2))
                    return last
                return mms

            def project(weights, src):
                return lambda c: lambda bank: pe.matmul(bank, weights, src[:, c * CH:(c + 1) * CH],
                                                        start=True, stop=True)

            def values(c):
                def mms(bank):
                    for i in range(TC):
                        t = c * TC + i
                        last = pe.matmul(bank[:, i * P:(i + 1) * P], xcT[:, t * P:(t + 1) * P],
                                         mat("qkv")[:, 2 * P:3 * P], start=True, stop=True)
                    return last
                return mms

            def first(step, c, mms):
                mms(PS[:, bank_of(PA_MM.n(step, c)), :]).then_inc(pa_mm, 1)

            pe.wait_ge(consts_set, 1)
            for c in range(C):
                first("T", c, transposes(c))
            for c in range(C):
                first("X", c, conv(c))
            for c in range(C):
                pe.wait_ge(pa_act, PA_ACT.n("X", c))
                first("Q", c, project(mat("qkv")[:, 0:P], xcT)(c))
            for c in range(C):
                first("K", c, project(mat("qkv")[:, P:2 * P], xcT)(c))
            for c in range(C):
                pe.wait_ge(pa_dve, PA_DVE.n("Q", c))
                first("V", c, values(c))
            for c in range(2 * C):
                pe.wait_ge(pa_dve, PA_DVE.n("K", c) if c < C else PA_DVE.n("V", c - C))
                at = c % 2 * P
                first("GD", c, project(mat("gru")[:, at:at + P], xnT[:, 1:N + 1])(c // 2))

            def slot(h):
                return (h % RING) * N

            def maxima_tile(mh, k, i):
                unit = mh * T + k
                if i % 2 == 0 and not (isinstance(mh, int) and unit == 0):
                    pe.wait_ge(mx_used, 2 * unit + i // 2 - 1)
                mm = pe.matmul(PS[:, MB + i, :], q_ring[0:MROW, bass.ds(slot(mh) + k * P, P)],
                               k_ring[0:MROW, bass.ds(slot(mh) + i * CH, CH)], start=True, stop=True)
                if i % 2 == 1:
                    mm.then_inc(mx_ready, 1)

            def scores_tile(h, k, i):
                if not (isinstance(h, int) and h == 0 and k == 0 and i < 2):
                    pe.wait_ge(exp_done, (h * T + k) * C + i - 1)
                pe.matmul(PS[:, SB + i % 2, :], k_ring[0:KS, bass.ds(slot(h) + k * P, P)],
                          q_ring[0:KS, bass.ds(slot(h) + i * CH, CH)], start=True, stop=True).then_inc(s_ready, 1)

            def weigh_values(h, k):
                pe.wait_ge(exp_done, (h * T + k) * C + C)
                if k == 0:
                    pe.wait_ge(v_ready, h + 1)
                    if not (isinstance(h, int) and h == 0):
                        pe.wait_ge(o_copied, h)
                for i in range(C):
                    mm = pe.matmul(PS[VW * i:VW * (i + 1), PVB, :], Vh[:, k, :], probs[:, C * (k % 2) + i, :],
                                   start=(k == 0), stop=(k == T - 1))
                mm.then_inc(pv_done, 1)

            def turn_maxima(m, outputs):
                pe.wait_ge(mp_ready, m + 1)
                if not (isinstance(m, int) and m == 0):
                    pe.wait_ge(mt_copied, m)
                if outputs is not None:
                    pe.wait_ge(o_used, outputs)
                pe.transpose(PS[0:PARTS * TC, MISC, 0:P // 2].bitcast(BF16),
                             m_parts[:, :, :].rearrange("p a t -> p (a t)"), ident_bf[:, :]).then_inc(mt_ready, 1)

            def turn_output(h, m):
                pe.wait_ge(o_copied, h + 1)
                if m is not None:
                    pe.wait_ge(mt_copied, m)
                for i in range(TC):
                    mm = pe.transpose(PS[:, MISC, i * P:(i + 1) * P], o_sum[:, i * P:(i + 1) * P], ident)
                mm.then_inc(ot_ready, 1)

            def pair(h, k, with_maxima):
                if k == 0:
                    pe.wait_ge(m_rows, 16 * C * (h + 1))
                mh, mk = h + (k + T + C) // T, (k + C) % T
                if with_maxima and mk == 0:
                    pe.wait_ge(heads_in, 96 * mh)
                for i in range(C):
                    scores_tile(h, k, i)
                    if with_maxima:
                        maxima_tile(mh, mk, i)

            def head(h, first_head, last):
                for k in range(T):
                    if k < T - 1:
                        pair(h, k + 1, last > 1 or (last == 1 and k + 1 < T - C))
                    elif last > 0:
                        pair(h + 1, 0, last > 1)
                    weigh_values(h, k)
                    if k % C == 1 and last > 0:
                        turn_maxima(C * (h + 1) + k // C, None if first_head else h - 1 if k < C else h)
                    if k == C - 1 and not first_head:
                        turn_output(h - 1, C * (h + 1) + 1 if last > 0 else C * H)

            pe.wait_ge(pa_act, PA_ACT.total)
            pe.wait_ge(pa_dve, PA_DVE.total)
            pe.wait_ge(identb_set, 1)
            pe.wait_ge(head0_in, 96)
            for unit in range(T + C):
                if unit == T:
                    pe.wait_ge(heads_in, 96 * 2)
                for i in range(C):
                    maxima_tile(unit // T, unit % T, i)
                if unit % C == C - 1 and unit > C:
                    turn_maxima(unit // C - 1, None)
            pair(0, 0, True)
            head(0, True, H - 1)
            with pe.Fori(1, H - 2) as h:
                head(h, False, 2)
            head(H - 2, False, 1)
            head(H - 1, False, 0)
            pe.wait_ge(o_used, H - 1)
            turn_output(H - 1, None)
            pe.wait_ge(o_used, H)
            pe.wait_ge(mx_used, 8 * H * C)
            pe.wait_ge(mats2_in, 16)
            pe.wait_ge(small_in, 48)

            def fill(step, c, mms):
                mms(PS[:, bank_of(C_MM.n(step, c)), :]).then_inc(c_mm, 1)

            def turn_tiles(src, ready=None):
                def mms(bank):
                    for i in range(TC):
                        last = pe.transpose(bank[:, i * P:(i + 1) * P], src(i), ident)
                    return last
                return mms

            for c in range(C):
                fill("U", c, turn_tiles(lambda i: ctx_sb[:, c * TC + i, :]))
            for c in range(C):
                def mms(bank):
                    for i in range(TC):
                        at = slice((c * TC + i) * P, (c * TC + i + 1) * P)
                        pe.matmul(bank[:, i * P:(i + 1) * P], ctxT[:, at], mat("wo"), start=True, stop=False)
                        last = pe.matmul(bank[:, i * P:(i + 1) * P], xcT[:, at], ident, start=False, stop=True)
                    return last
                pe.wait_ge(c_act, C_ACT.n("U", c))
                fill("O", c, mms)
            for c in range(C):
                pe.wait_ge(ln1_done, c + 1)
                pe.wait_ge(c_act, C_ACT.n("U", c))
                fill("Y", c, turn_tiles(lambda i: x1[:, c * TC + i, :]))

            def gate(bank):
                for t in range(T):
                    last = pe.matmul(bank[:, t * E0:(t + 1) * E0], x1T[:, t * P:(t + 1) * P], mat("gate"),
                                     start=True, stop=True)
                return last
            pe.wait_ge(c_act, C_ACT.n("Y"))
            pe.wait_ge(c_dve, C_DVE.n("O"))
            fill("G", 0, gate)
            pe.wait_ge(pp_ready, 1)
            for c in range(C):
                def mms(bank):
                    for i in range(TC):
                        last = pe.transpose(bank[0:E0, i * P:(i + 1) * P], gate_p[:, c * TC + i, :], ident)
                    return last
                pe.wait_ge(c_dve, C_DVE.n("O"))
                fill("p", c, mms)
            pe.wait_ge(pp_ready, 2)
            for c in range(2):
                def mms(bank):
                    for i in range(2 * TC):
                        last = pe.transpose(bank[0:PARTS * PICK, i * P // 2:(i + 1) * P // 2].bitcast(BF16),
                                            gate_parts[:, c * 2 * TC + i, :], ident_bf[:, :])
                    return last
                fill("s", c, mms)

            pe.wait_ge(c_act, C_ACT.total)
            pe.wait_ge(c_dve, C_DVE.total)
            for c in range(C):
                pe.matmul(PS[:, c, :], b2_sb[:, :], pT[:, c * CH:(c + 1) * CH], start=True, stop=False)

            def spread(e, c):
                if not (isinstance(e, int) and e == 0 and c < 2):
                    pe.wait_ge(h_dve, (e * C + c - 1) * FT)
                pe.matmul(PS[:, PB + c % 2, :], pick_sb[:, bass.ds(e * P, P)], p_stack[:, c * CH:(c + 1) * CH],
                          start=True, stop=True).then_inc(p_mm, 1)

            def hidden(e, par, c, f, loads):
                unit = (e * C + c) * FT + f
                if c == 0 and f == 0:
                    pe.wait_ge(w1_in[par], 16 * loads)
                if f == 0:
                    spread(e, c)
                if not (isinstance(e, int) and unit < 2):
                    pe.wait_ge(h_act, unit - 1)
                pe.matmul(PS[:, HB + f % 2, :], w1_buf[:, par, f * P:(f + 1) * P], x1T[:, c * CH:(c + 1) * CH],
                          start=True, stop=True).then_inc(h_mm, 1)

            def add_up(e, par, c, f, loads, last):
                unit = (e * C + c) * FT + f
                if c == 0 and f == 0:
                    pe.wait_ge(w2_in[par], 16 * loads)
                pe.wait_ge(h_dve, unit + 1)
                pe.matmul(PS[:, c, :], w2_buf[:, par, f * P:(f + 1) * P], h_wt[:, f, :],
                          start=False, stop=last and f == FT - 1).then_inc(y_mm, 1)

            def experts(pair, final):
                per = C * FT
                for u in range(2 * per):
                    n = u + 2
                    if n < 2 * per:
                        hidden(2 * pair + n // per, n // per, n % per // FT, n % FT, pair + 1)
                    elif not final:
                        hidden(2 * pair + 2, 0, 0, n - 2 * per, pair + 2)
                    add_up(2 * pair + u // per, u // per, u % per // FT, u % FT, pair + 1,
                           final and u >= per)

            hidden(0, 0, 0, 0, 1)
            hidden(0, 0, 0, 1, 1)
            experts(0, False)
            with pe.Fori(1, E0 // 2 - 1) as pair_of:
                experts(pair_of, False)
            experts(E0 // 2 - 1, True)
            def fill(step, c, mms):
                mms(PS[:, bank_of(E_MM.n(step, c) + C), :]).then_inc(e_mm, 1)

            pe.wait_ge(h_dve, E0 * C * FT)
            for c in range(C):
                pe.wait_ge(r_dve, c + 1)
                fill("R", c, turn_tiles(lambda i: ctxT[:, (c * TC + i) * P:(c * TC + i + 1) * P]))
            for c in range(C):
                fill("S", c, turn_tiles(lambda i: sT[:, (c * TC + i) * P:(c * TC + i + 1) * P]))

            def fill(step, c, mms):
                mms(PS[:, bank_of(D_MM.n(step, c)), :]).then_inc(d_mm, 1)

            pe.wait_ge(e_act, C)
            pe.wait_ge(e_dve, C)
            for c in range(C):
                pe.wait_ge(norm3, (c + 1) * TC)
                fill("A", c, turn_tiles(lambda i: xn2[:, c * TC + i, :]))

            def logits(bank):
                for t in range(T):
                    last = pe.matmul(bank[:, t * E1:(t + 1) * E1], xn2T[:, t * P:(t + 1) * P], mat("wr"),
                                     start=True, stop=True)
                return last
            pe.wait_ge(d_act, D_ACT.n("A"))
            fill("L", 0, logits)
            for c in range(C):
                pe.wait_ge(h_norm, (c + 1) * TC)
                fill("B", c, turn_tiles(lambda i: hN[:, c * TC + i, :]))

            def from_h(part, c):
                return lambda bank: pe.matmul(bank, mat("win")[:, part * P:(part + 1) * P],
                                              hT[:, c * CH:(c + 1) * CH], start=True, stop=True)
            for c in range(C):
                pe.wait_ge(d_act, D_ACT.n("B", c))
                if c == C - 1:
                    pe.wait_ge(d_dve, D_DVE.n("L"))
                fill("U", c, from_h(0, c))
            for c in range(C):
                fill("U", C + c, from_h(1, c))

            def count(bank):
                m = mask[:, :, :].rearrange("p t e -> p (t e)")
                pe.matmul(bank[:, 0:T * E1], tri_bf[:, 0:P], m, start=True, stop=True)
                return pe.matmul(bank[:, T * E1:2 * T * E1], tri_bf[:, P:2 * P], m, start=True, stop=True)
            pe.wait_ge(mask_set, 1)
            pe.wait_ge(d_act, D_ACT.n("U", 0))
            fill("K", 0, count)
            for j in range(2):
                for c in range(C):
                    def mms(bank):
                        for i in range(2):
                            at = (i * 2 + j) * P
                            last = pe.matmul(bank, mat("wdt")[:, at:at + P], u[i][:, c * CH:(c + 1) * CH],
                                             start=(i == 0), stop=(i == 1))
                        return last
                    i = j * C + c
                    if j == 0:
                        pe.wait_ge(d_act, D_ACT.n("U", C + c))
                    if i == 2 * C - 1:
                        pe.wait_ge(d_dve, D_DVE.n("K"))
                    fill("M", i, mms)
            for j in range(2):
                for c in range(C):
                    pe.wait_ge(d_act, D_ACT.n("M", j * C + c))
                    fill("Z", j * C + c, from_h(2 + j, c))
            for c in range(C):
                def mms(bank):
                    for i in range(TC):
                        at = slice((c * TC + i) * P, (c * TC + i + 1) * P)
                        for j in range(2):
                            last = pe.matmul(bank[:, i * P:(i + 1) * P], lam[j][:, at],
                                             mat("wout")[:, j * P:(j + 1) * P], start=(j == 0), stop=(j == 1))
                    return last
                pe.wait_ge(z_used, C + c + 1)
                pe.wait_ge(d_act, D_ACT.n("Z", c))
                fill("Y", c, mms)

            def expert(n):
                return pe.value_load(te_i[0:1, bass.ds(n, 1)], min_val=0, max_val=E1 - 1)

            def turn_slots(n, k, loads):
                pe.wait_ge(xt_in[k % 4], 16 * loads)
                if not (isinstance(n, int) and n == 0):
                    pe.wait_ge(xt_act, n)
                pe.transpose(PS[:, XB, 0:P], xt[:, k % 4, :], ident).then_inc(xt_mm, 1)

            def hidden_slots(n, k):
                e = expert(n)
                pe.wait_ge(xt_act, n + 1)
                if not (isinstance(n, int) and n < 2):
                    pe.wait_ge(g_dve, n - 1)
                for b, w in ((H1B, 0), (H3B, F1)):
                    mm = pe.matmul(PS[:, b + k % 2, :], xtT[:, k % 4, :], big[:, bass.ds(e * W_ALL + w, F1)],
                                   start=True, stop=True)
                mm.then_inc(g_mm, 1)

            def turn_hidden(n, k):
                pe.wait_ge(g_dve, n + 1)
                if not (isinstance(n, int) and n == 0):
                    pe.wait_ge(gt_act, n)
                for f in range(F1 // P):
                    mm = pe.transpose(PS[:, GB, f * P:(f + 1) * P], hid[:, k % 2, f * P:(f + 1) * P], ident)
                mm.then_inc(gt_mm, 1)

            def outputs(n, k):
                e = expert(n)
                pe.wait_ge(gt_act, n + 1)
                if not (isinstance(n, int) and n < 2):
                    pe.wait_ge(yt_dve, n - 1)
                for f in range(F1 // P):
                    mm = pe.matmul(PS[:, YB + k % 2, 0:P], hidT[:, k % 2, f * P:(f + 1) * P],
                                   big[:, bass.ds(e * W_ALL + 2 * F1 + f * P, P)],
                                   start=(f == 0), stop=(f == F1 // P - 1))
                mm.then_inc(yt_mm, 1)

            def experts_pe(b, first, last):
                for k in range(LOOP):
                    n = LOOP * b + k
                    if not (last and k == LOOP - 1):
                        hidden_slots(n + 1, k + 1)
                    if not (first and k == 0):
                        outputs(n - 1, k + 1)
                    turn_hidden(n, k)
                    if not (last and k >= LOOP - 2):
                        turn_slots(n + 2, k + 2, 2 * b + 1 + (k + 2) // 4)

            pe.wait_ge(d_act, D_ACT.total)
            pe.wait_ge(d_dve, D_DVE.total)
            pe.wait_ge(te_set, 1)
            pe.wait_ge(wall_in, 64)
            turn_slots(0, 0, 1)
            turn_slots(1, 1, 1)
            hidden_slots(0, 0)
            experts_pe(0, True, False)
            with pe.Fori(1, NT // LOOP - 1) as b:
                experts_pe(b, False, False)
            experts_pe(NT // LOOP - 1, False, True)
            outputs(NT - 1, 1)


_OUTS = [((N, P), "float32")]


def kernel(**inputs):
    import ml_dtypes
    import numpy as np
    import concourse.bacc as bacc
    from concourse.bass_utils import run_bass_kernel_spmd as run

    g = {k: np.asarray(v) for k, v in inputs.items()}

    def tiles(w):
        *lead, k, n = w.shape
        w = w.reshape(*lead, k // P, P, n)
        return np.ascontiguousarray(np.swapaxes(w, -3, -2)).reshape(*lead, P, k // P * n)

    mats = {"gru": g["L0_attn_W"].T, "conv": g["L0_ffn_conv_w"].transpose(1, 2, 0).reshape(P, 3 * P),
            "qkv": g["L0_ffn_wqkv"].T, "ident": np.eye(P, dtype=np.float32), "wo": g["L0_ffn_wo"].T,
            "gate": g["L0_ffn_gate_w"], "wr": g["L1_ffn_Wr"], "win": g["L1_attn_W_in"].T,
            "wdt": tiles(g["L1_attn_W_dt"].T), "wout": tiles(g["L1_attn_W_out"].T)}
    bqkv = g["L0_ffn_bqkv"].reshape(3, P)
    cols = {"conv_b": g["L0_ffn_conv_b"][:, None], "bq": bqkv[0][:, None], "bk": bqkv[1][:, None],
            "b1": g["L0_ffn_b1"].reshape(E0 * FT, P).T, "b_dt": g["L1_attn_b_dt"].reshape(2, P).T,
            "w_norm": g["L1_attn_w_norm"][:, None]}
    rows = {"bv": bqkv[2], "bo": g["L0_ffn_bo"], "ln1_g": g["L0_ffn_ln1_g"], "ln1_b": g["L0_ffn_ln1_b"],
            "ln2_g": g["L0_ffn_ln2_g"], "ln2_b": g["L0_ffn_ln2_b"], "gate_b": g["L0_ffn_gate_b"],
            "br": g["L1_ffn_br"], "gamma": g["L1_ffn_gamma"].reshape(-1), "iota": np.arange(NT, dtype=np.float32),
            "beta": g["L1_ffn_beta"].reshape(-1)}
    w_all = np.concatenate([g["L1_ffn_W1"], g["L1_ffn_W3"], tiles(g["L1_ffn_W2"])], axis=2)
    pick = np.zeros((PARTS, PICK, E0, P), np.uint16)
    for e in range(E0):
        pick[:, e, e] = 0x3F80
    arrays = {
        "x": g["L0_attn_x"].reshape(N, P),
        "mats": np.concatenate([mats[k] for k in MATS], axis=1),
        "cols": np.concatenate([cols[k] for k in COLS], axis=1),
        "rows": np.concatenate([rows[k] for k in ROWS]),
        "b2": g["L0_ffn_b2"], "pick": pick.reshape(PARTS * PICK, E0 * P).view(ml_dtypes.bfloat16),
        "w1": g["L0_ffn_w1"], "w2": tiles(g["L0_ffn_w2"]),
        "tri": np.concatenate([np.triu(np.ones((P, P), ml_dtypes.bfloat16), 1),
                               np.ones((P, P), ml_dtypes.bfloat16)], axis=1),
        "w_all": w_all.transpose(1, 0, 2).reshape(P, E1 * W_ALL),
    }
    nc = bacc.Bacc("TRN2", target_bir_lowering=False, num_devices=1)
    feeds, args = {}, {}
    for name, a in arrays.items():
        a = np.ascontiguousarray(a)
        feeds[f"in_{name}"] = a
        args[name] = nc.dram_tensor(f"in_{name}", a.shape, mybir.dt.from_np(a.dtype), kind="ExternalInput").ap()
    args["out"] = nc.dram_tensor("out_0", [N, P], F32, kind="ExternalOutput").ap()
    build(nc, **args)
    r = run(nc, [feeds], core_ids=[0])
    return r.results[0]["out_0"].reshape(1, N, P)
```

```python
from contextlib import ExitStack

import concourse.bass as bass
from concourse import mybir

ALU = mybir.AluOpType
ACT = mybir.ActivationFunctionType
AX = mybir.AxisListType
F32 = mybir.dt.float32
BF16 = mybir.dt.bfloat16
U32 = mybir.dt.uint32

P = 128
N = 2048
T = N // P
CH = 512
C = N // CH
TC = CH // P
EPS = 1e-5

H = 16
DH = P // H
PARTS = 3
STACK = PARTS * PARTS * DH
MROW = 96
KS = MROW + PARTS
RING = 4
VW = 32

E0, F0 = 8, 512
E1, F1 = 16, 512
FT = F0 // P
LOOP = 8
NT = LOOP * -(-((2 * N + (P - 1) * E1) // P) // LOOP)
ROW_W = P + 2
INNER = 2 * P

MATS = {}
_at = 0
for _name, _w in (("ident", P), ("conv", 3 * P), ("qkv", 3 * P), ("gru", 2 * P),
                  ("wo", P), ("gate", E0), ("wr", E1), ("win", 2 * INNER), ("wdt", 2 * INNER),
                  ("wout", 2 * P)):
    MATS[_name] = (_at, _at + _w)
    _at += _w
MATS_W = _at
MATS_1 = MATS["gru"][1]
COLS = {}
_at = 0
for _name, _w in (("conv_b", 1), ("bq", 1), ("bk", 1), ("b1", E0 * FT), ("b_dt", 2), ("w_norm", 1),
                  ("ln1_g", 1), ("ln1_b", 1), ("token", T), ("spare", NT)):
    COLS[_name] = (_at, _at + _w)
    _at += _w
COLS_W = _at
ROWS = {}
_at = 0
for _name, _w in (("bv", P), ("bo", P), ("ln2_g", P), ("ln2_b", P),
                  ("gate_b", E0), ("br", E1), ("iota", NT)):
    ROWS[_name] = (_at, _at + _w)
    _at += _w
ROWS_W = _at
W_ALL = 3 * F1
PICK = 32


class Chain:

    def __init__(self, eng, sem):
        self.eng, self.sem, self.base, self.n = eng, sem, 0, 0

    def did(self, ins):
        ins.then_inc(self.sem, 1)
        self.n += 1

    def settle(self):
        self.eng.wait_ge(self.sem, self.base + self.n)

    def step(self, ins):
        self.did(ins)
        self.settle()

    def total(self):
        return self.base + self.n

    def at(self, count):
        self.base, self.n = count, 0


class Steps:

    def __init__(self, **steps):
        self.banks, self.before, at = steps, {}, 0
        for name, n in steps.items():
            self.before[name] = at
            at += n
        self.total = at

    def n(self, step, c=None):
        return self.before[step] + (self.banks[step] if c is None else c + 1)


def bank_of(n):
    return (n - 1) % 8


def build(nc, x, mats, cols, rows, b2, gains, pick, tri, w1, w2, w_all, out):
    with ExitStack() as ctx:
        def sb(name, shape, dt=F32):
            return ctx.enter_context(nc.sbuf_tensor(name, shape, dt))

        def sem(name):
            return ctx.enter_context(nc.semaphore(name))

        x_sb = sb("x_sb", [P, T, P])
        xn_rows = sb("xn_rows", [P, T, ROW_W])
        xn = xn_rows[:, :, 0:P]
        xnT = sb("xnT", [P, N + 2])
        sT = sb("sT", [P, N])
        xcT = sb("xcT", [P, N])
        big = sb("big", [P, E1 * W_ALL])
        qf = big[:, 0:N]
        kf = big[:, N:2 * N]
        qparts = big[:, 2 * N:4 * N - N // 2].bitcast(BF16).rearrange("p (a n) -> p a n", a=PARTS)
        kparts = big[:, 4 * N - N // 2:5 * N].bitcast(BF16).rearrange("p (a n) -> p a n", a=PARTS)
        q_ring = big[:, 5 * N:7 * N].bitcast(BF16)
        k_ring = big[:, 7 * N:9 * N].bitcast(BF16)
        probs_f = big[:, 9 * N:11 * N]
        probs = probs_f.rearrange("p (s q) -> p s q", s=8)
        V = big[:, 11 * N:12 * N].rearrange("p (t d) -> p t d", t=T)
        Vo = sb("Vo", [P, T * VW + CH])
        Vh = Vo[:, 0:T * VW].rearrange("p (t w) -> p t w", t=T)
        o_sum = Vo[:, T * VW:T * VW + CH]
        tmpT = sb("tmpT", [P, N])
        ctx_sb = sb("ctx_sb", [P, T, P])
        mat_sb = sb("mat_sb", [P, MATS_W])
        col_sb = sb("col_sb", [P, COLS_W])
        row_sb = sb("row_sb", [P, ROWS_W])
        b2_sb = sb("b2_sb", [E0, P])
        gains_sb = sb("gains_sb", [2 * E1, 3 * P])
        pick_sb = sb("pick_sb", [PARTS * PICK, E0 * P], BF16)
        w1_buf = sb("w1_buf", [P, 2, F0])
        w2_buf = sb("w2_buf", [P, 2, F0])
        ident_bf = sb("ident_bf", [P, P], BF16)
        stats = sb("stats", [P, T, 6])
        moments = sb("moments", [P, T, 2])
        rstd = sb("rstd", [P, T])
        mx = sb("mx", [P, 2, 8])
        neg_m = sb("neg_m", [P, TC])
        m_rest = sb("m_rest", [P, TC])
        m_parts = sb("m_parts", [P, PARTS, TC], BF16)
        zeros = sb("zeros", [P, TC])
        mT = sb("mT", [PARTS * TC, P], BF16)
        o_inv = sb("o_inv", [P, T])
        sig_h, gate_z, gate_c = probs_f[:, 0:N], probs_f[:, N:2 * N], tmpT
        ctxT = tmpT
        x1 = xn
        x1T = xnT[:, 0:N]
        gate_p = sb("gate_p", [P, T, E0])
        gate_rest = sb("gate_rest", [P, T, E0])
        gate_s = sb("gate_s", [P, T])
        gate_parts = sb("gate_parts", [P, T, PARTS * PICK], BF16)
        p_stack = xcT[0:PARTS * PICK, 0:N // 2].bitcast(BF16)
        h_relu = xcT[:, N // 2:N].rearrange("p (s q) -> p s q", s=2)
        h_wt = ctx_sb[:, :, :].rearrange("p t d -> p (t d)").rearrange("p (s q) -> p s q", s=4)
        pT = tmpT[0:E0, :]
        xn2 = xn
        xn2T = tmpT
        hN = ctx_sb
        hT = xnT[:, 0:N]
        u = [sT, xcT]
        lam = [tmpT, ctx_sb[:, :, :].rearrange("p t d -> p (t d)")]
        z_tmp = [w1_buf[:, 0, :], w1_buf[:, 1, :], w2_buf[:, 0, :], w2_buf[:, 1, :]]
        s1 = sT[:, :].rearrange("p (t d) -> p t d", t=T)
        y1 = xcT[:, :].rearrange("p (t d) -> p t d", t=T)
        y2 = tmpT[:, :].rearrange("p (t d) -> p t d", t=T)
        tri_bf = sb("tri_bf", [P, 2 * P], BF16)
        rms = sb("rms", [P, T])
        route = w1_buf[:, :, :].rearrange("p a f -> p (a f)")
        rp, place = (route[:, i * T * E1:(i + 1) * T * E1].rearrange("p (t e) -> p t e", t=T) for i in range(2))
        tot, upto = (route[:, i * T * E1:(i + 1) * T * E1].rearrange("p (e t) -> p e t", t=T) for i in range(2, 4))
        rs = sb("rs", [P, T])
        top = sb("top", [P, T, 8])
        top_i = sb("top_i", [P, T, 8], U32)
        top_f = sb("top_f", [P, 2, T])
        wgt = sb("wgt", [P, 2, T])
        hot = w2_buf[:, 0, :].rearrange("p (k t e) -> p k t e", k=2, t=T)
        hot_w = sb("hot_w", [P, T, 2 * E1])
        hot_wT = ctx_sb[0:2 * E1, :, :].rearrange("p t d -> p (t d)")
        mask = sb("mask", [P, T, E1], BF16)
        reset = sb("reset", [P, E1, T])
        n_tiles = sb("n_tiles", [P, E1])
        end = sb("end", [P, E1])
        pos = sb("pos", [P, 2, T])
        pos_i = sb("pos_i", [P, 2, T], U32)
        te_thr = sb("te_thr", [P, T])
        te = sb("te", [P, NT])
        other = sb("other", [P, 4])
        dest_f = sb("dest_f", [P, NT])
        dest = sb("dest", [P, LOOP], U32)
        te_i = sb("te_i", [1, NT], U32)
        te_cmp = hN[:, 0:NT * E1 // P, :].rearrange("p a b -> p (a b)").rearrange("p (t e) -> p t e", e=E1)
        xt = gate_parts[:, :, :].rearrange("p t w -> p (t w)").bitcast(F32)[:, 0:4 * ROW_W]\
            .rearrange("p (s w) -> p s w", s=4)
        xtT = w1_buf[:, 1, :].rearrange("p (s d) -> p s d", s=4)
        hid = Vo[:, 0:2 * CH].rearrange("p (s f) -> p s f", s=2)
        hidT = w2_buf
        y_ring = xnT[:, 0:LOOP * P].rearrange("p (s d) -> p s d", s=LOOP)
        y_mom = sb("y_mom", [P, LOOP, 2])
        y_st = sb("y_st", [P, LOOP, 6])
        y_rstd = sb("y_rstd", [P, LOOP])
        FILL = NT // 4
        spare = col_sb[:, COLS["spare"][0]:COLS["spare"][1]]
        empty = ctx_sb[:, :, :].rearrange("p t d -> p (t d)")[:, 0:FILL * ROW_W].rearrange("p (n w) -> p n w", w=ROW_W)
        xg_dram = nc.dram_tensor("xg_dram", [NT * P, ROW_W], F32, kind="Internal").ap()
        yt_dram = nc.dram_tensor("yt_dram", [3 * N + NT * P, P], F32, kind="Internal").ap()
        PS = ctx.enter_context(nc.psum_tensor("PS", [P, 8, CH], F32))
        parts_dram = nc.dram_tensor("parts_dram", [2, PARTS, P, N], BF16, kind="Internal").ap()

        def mat(name):
            return mat_sb[:, MATS[name][0]:MATS[name][1]]

        def col(name, i=0):
            return col_sb[:, COLS[name][0] + i:COLS[name][0] + i + 1]

        def row(name):
            return row_sb[:, ROWS[name][0]:ROWS[name][1]]

        ident = mat("ident")

        x_in = [sem(f"x_in{c}") for c in range(C)]
        ident_in = sem("ident_in")
        mats_in = sem("mats_in")
        edges_set = sem("edges_set")
        mats2_in = sem("mats2_in")
        cols_in = sem("cols_in")
        rows_in = sem("rows_in")
        consts_set = sem("consts_set")
        act_chain = sem("act_chain")
        dve_chain = sem("dve_chain")
        pool_chain = sem("pool_chain")
        ln_var = sem("ln_var")
        ln_std = sem("ln_std")
        xn_ready = sem("xn_ready")
        pa_mm = sem("pa_mm")
        pa_act = sem("pa_act")
        pa_dve = sem("pa_dve")
        gru_sig = sem("gru_sig")
        full_set = sem("full_set")
        split_q = sem("split_q")
        split_k = sem("split_k")
        parts_out = sem("parts_out")
        heads_in = sem("heads_in")
        s_ready = sem("s_ready")
        exp_done = sem("exp_done")
        mx_ready = sem("mx_ready")
        mx_used = sem("mx_used")
        mx_chunk = sem("mx_chunk")
        mp_ready = sem("mp_ready")
        mt_ready = sem("mt_ready")
        mt_copied = sem("mt_copied")
        m_rows = sem("m_rows")
        v_ready = sem("v_ready")
        pv_done = sem("pv_done")
        o_copied = sem("o_copied")
        ot_ready = sem("ot_ready")
        o_used = sem("o_used")
        out_done = sem("out_done")
        head0_in = sem("head0_in")
        small_in = sem("small_in")
        w1_in = [sem("w1_in0"), sem("w1_in1")]
        w2_in = [sem("w2_in0"), sem("w2_in1")]
        c_mm = sem("c_mm")
        c_act = sem("c_act")
        c_dve = sem("c_dve")
        bias_seen = sem("bias_seen")
        ln1_done = sem("ln1_done")
        probs_exp = sem("probs_exp")
        pp_ready = sem("pp_ready")
        h_mm = sem("h_mm")
        h_act = sem("h_act")
        h_dve = sem("h_dve")
        p_mm = sem("p_mm")
        y_mm = sem("y_mm")
        r_dve = sem("r_dve")
        wall_in = sem("wall_in")
        zero_out = sem("zero_out")
        norm3 = sem("norm3")
        rms_sum = sem("rms_sum")
        rms_root = sem("rms_root")
        rms_inv = sem("rms_inv")
        h_norm = sem("h_norm")
        route_exp = sem("route_exp")
        mask_set = sem("mask_set")
        pos_set = sem("pos_set")
        hot_w_set = sem("hot_w_set")
        te_set = sem("te_set")
        scattered = sem("scattered")
        d_mm = sem("d_mm")
        d_act = sem("d_act")
        d_dve = sem("d_dve")
        u_gated = sem("u_gated")
        z_used = sem("z_used")
        s_gated = sem("s_gated")
        xt_in = [sem(f"xt_in{i}") for i in range(4)]
        xt_mm = sem("xt_mm")
        xt_act = sem("xt_act")
        g_mm = sem("g_mm")
        g_act = sem("g_act")
        g_dve = sem("g_dve")
        gt_mm = sem("gt_mm")
        gt_act = sem("gt_act")
        yt_mm = sem("yt_mm")
        yt_dve = sem("yt_dve")
        y_var = sem("y_var")
        y_std = sem("y_std")
        y_norm = sem("y_norm")
        other_set = sem("other_set")
        dest_set = sem("dest_set")
        y_out = sem("y_out")
        rows_back = [sem(f"rows_back{c}") for c in range(C)]
        hot_mm = sem("hot_mm")
        hot_act = sem("hot_act")
        shift_mm = sem("shift_mm")
        shift_act = sem("shift_act")
        gain_mm = sem("gain_mm")
        mixed = sem("mixed")
        silu1 = sem("silu1")
        done = sem("done")
        e_mm = sem("e_mm")
        e_act = sem("e_act")
        e_dve = sem("e_dve")
        norm2_tiles = sem("norm2_tiles")
        norm2 = sem("norm2")
        silu0 = sem("silu0")
        x_ready = sem("x_ready")
        identb_set = sem("identb_set")

        block = ctx.enter_context(nc.Block())

        PA_MM = Steps(T=C, X=C, Q=C, K=C, V=C, GD=2 * C)
        PA_ACT = Steps(T=C, X=C, Q=C, K=C, GD=2 * C)
        PA_DVE = Steps(V=C)
        C_MM = Steps(U=C, O=C, Y=C, G=1, p=C, s=2)
        C_ACT = Steps(U=C, Y=C, p=C, s=2)
        C_DVE = Steps(O=C, G=1)
        HB, PB = 4, 6
        E_MM = Steps(R=C, S=C)
        D_MM = Steps(A=C, L=1, B=C, U=2 * C, K=1, M=2 * C, Z=2 * C, Y=C)
        D_ACT = Steps(A=C, B=C, U=2 * C, M=2 * C, Z=2 * C)
        D_DVE = Steps(L=1, K=1, Y=C)
        H1B, H3B, GB, XB, YB = 0, 2, 4, 5, 6
        SCORES_ORDER = [("scores", 0), ("scores", 1), ("maxima", 0), ("maxima", 1), ("maxima", 2), ("scores", 2),
                        ("maxima", 3), ("scores", 3)]
        SB, MB, PVB, MISC = 0, 2, 6, 7

        def scores_bank(h, i):
            return SB + (i if isinstance(h, int) and h == H - 1 else i % 2)

        def chunk_shift(c):
            return big[:, c * CH:(c + 1) * CH].rearrange("p (t d) -> p t d", t=TC)

        def d_free(eng):
            eng.wait_ge(z_used, 2 * C)

        @block.sync
        def _(sp):
            xv = x.rearrange("(t p) d -> p t d", p=P)
            for c in range(C):
                sp.dma_start(x_sb[:, c * TC:(c + 1) * TC, :], xv[:, c * TC:(c + 1) * TC, :]).then_inc(x_in[c], 16)
            sp.wait_ge(mats_in, 16)
            sp.dma_start(mat_sb[:, MATS_1:MATS_W], mats[:, MATS_1:MATS_W]).then_inc(mats2_in, 16)
            sp.dma_start(b2_sb[:, :], b2[:, :]).then_inc(small_in, 16)
            sp.dma_start(gains_sb[:, :], gains[:, :]).then_inc(small_in, 16)
            sp.dma_start(pick_sb[:, :], pick[:, :]).then_inc(small_in, 16)
            sp.dma_start(tri_bf[:, :], tri[:, :]).then_inc(small_in, 16)
            for par in range(2):
                sp.dma_start(w1_buf[:, par, :], w1[par]).then_inc(w1_in[par], 16)
                sp.dma_start(w2_buf[:, par, :], w2[par]).then_inc(w2_in[par], 16)
            for who, (step, parts, ready) in enumerate((("Q", qparts, split_q), ("K", kparts, split_k))):
                sp.wait_ge(pa_act, PA_ACT.n(step))
                sp.dma_start(parts_dram[who, 0], parts[:, 0, :]).then_inc(parts_out, 16)
                for p in range(1, PARTS):
                    sp.wait_ge(ready, p)
                    sp.dma_start(parts_dram[who, p], parts[:, p, :]).then_inc(parts_out, 16)

            def load_head(h, landed):
                at = bass.ds((h % RING) * N, N)
                for a in range(PARTS):
                    rows_a = slice(a * PARTS * DH, (a + 1) * PARTS * DH)
                    sp.dma_start(q_ring[rows_a, at],
                                 parts_dram[0, a, bass.ds(h * DH, DH), :].partition_broadcast(PARTS))\
                        .then_inc(landed, 16)
                    sp.dma_start(k_ring[rows_a, at],
                                 parts_dram[1, :, bass.ds(h * DH, DH), :]).then_inc(landed, 16)

            def place_maxima(m):
                sp.wait_ge(mt_copied, m + 1)
                at = (m // C % RING) * N + (m % C) * CH
                sp.dma_start(q_ring[MROW:KS, bass.ds(at, CH)], mT[:, :]).then_inc(m_rows, 16)

            sp.wait_ge(parts_out, 16 * 2 * PARTS)
            sp.wait_ge(consts_set, 1)
            load_head(0, head0_in)
            load_head(1, heads_in)
            load_head(2, heads_in)
            for m in range(C):
                place_maxima(m)
            sp.wait_ge(heads_in, 96 * 2)
            load_head(3, heads_in)
            for m in range(C, 2 * C):
                place_maxima(m)
            with sp.Fori(1, H - RING + 1) as h:
                sp.wait_ge(pv_done, h * T)
                sp.wait_ge(heads_in, 96 * (h + 2))
                load_head(h + RING - 1, heads_in)
                with sp.Fori(0, C) as c:
                    place_maxima(C * (h + 1) + c)
            with sp.Fori(C * (H - RING + 2), C * H) as m:
                place_maxima(m)
            sp.wait_ge(o_used, H)
            sp.wait_ge(c_mm, 1)
            for k in range(4):
                w = E1 * W_ALL // 4
                sp.dma_start(big[:, k * w:(k + 1) * w], w_all[:, k * w:(k + 1) * w]).then_inc(wall_in, 16)
            for e in range(2, E0, 2):
                for par in range(2):
                    sp.wait_ge(h_mm, C * FT * (e + par - 1))
                    sp.dma_start(w1_buf[:, par, :], w1[e + par]).then_inc(w1_in[par], 16)
                    sp.wait_ge(y_mm, C * FT * (e + par - 1))
                    sp.dma_start(w2_buf[:, par, :], w2[e + par]).then_inc(w2_in[par], 16)
            sp.wait_ge(scattered, 16 * 2 * T)

            def load_tile(n, k):
                sp.dma_start(xt[:, k, :], xg_dram[bass.ds(n * P, P), :]).then_inc(xt_in[k], 16)

            for k in range(4):
                load_tile(k, k)
            for k in range(4):
                sp.wait_ge(xt_mm, k + 1)
                sp.wait_ge(dest_set, k + 1)
                load_tile(4 + k, k)
            with sp.Fori(1, NT // LOOP) as b:
                for half in range(2):
                    for k in range(4):
                        n = LOOP * b + 4 * half + k
                        sp.wait_ge(xt_mm, n - 3)
                        sp.wait_ge(dest_set, n - 3)
                        load_tile(n, k)
            d_free(sp)
            sp.wait_ge(s_gated, C)
            sp.wait_ge(y_out, 16 * NT)
            for c in range(C):
                for k, y in enumerate((y1, y2)):
                    at = k * N + c * CH
                    sp.dma_start(y[:, c * TC:(c + 1) * TC, :],
                                 yt_dram[at:at + CH, :].rearrange("(t p) d -> p t d", p=P)).then_inc(rows_back[c], 16)
            xo = out.rearrange("(t p) d -> p t d", p=P)
            for c in range(C):
                sp.wait_ge(done, c + 1)
                sp.dma_start(xo[:, c * TC:(c + 1) * TC, :], x_sb[:, c * TC:(c + 1) * TC, :]).then_inc(out_done, 16)
            sp.wait_ge(out_done, 16 * C)

        @block.gpsimd
        def _(pool):
            ch = Chain(pool, pool_chain)
            nc.gpsimd.memset(xnT[:, 0:1], 0.0).then_inc(edges_set, 1)
            pool.wait_ge(edges_set, 1)
            nc.gpsimd.memset(xnT[:, N + 1:N + 2], 0.0).then_inc(edges_set, 1)
            pool.wait_ge(edges_set, 2)
            ch.step(nc.gpsimd.memset(q_ring[64:MROW, :].bitcast(F32), 0.0))
            ch.step(nc.gpsimd.memset(k_ring[64:MROW, :].bitcast(F32), 0.0))
            ch.step(nc.gpsimd.memset(k_ring[MROW:KS, :], 1.0))
            nc.gpsimd.memset(zeros[:, :], 0.0).then_inc(consts_set, 1)
            pool.wait_ge(consts_set, 1)
            ch.step(nc.gpsimd.memset(Vh[:, :, :], 0.0))
            ch.step(nc.gpsimd.memset(Vh[:, :, DH:DH + 1], 1.0))
            nc.gpsimd.memset(gate_parts[:, :, :], 0.0).then_inc(consts_set, 1)
            pool.wait_ge(consts_set, 2)
            ch.step(nc.gpsimd.memset(reset[:, :, :], 1.0))
            ch.step(nc.gpsimd.memset(reset[:, :, 0:1], 0.0))
            ch.step(nc.gpsimd.memset(empty[:, :, :], 0.0))
            pool.wait_ge(cols_in, 16)
            ch.step(nc.gpsimd.memset(empty[:, :, P + 1:P + 2], -1.0))
            for k in range(NT // FILL):
                if k > 0:
                    pool.wait_ge(zero_out, 16 * k)
                ch.step(nc.gpsimd.tensor_copy(empty[:, :, P:P + 1], spare[:, k * FILL:(k + 1) * FILL].unsqueeze(2)))
                pool.dma_start(xg_dram.rearrange("(n p) d -> p n d", p=P)[:, k * FILL:(k + 1) * FILL, :],
                               empty[:, :, :]).then_inc(zero_out, 16)

            def copy_values(h):
                pool.wait_ge(consts_set, 1)
                nc.gpsimd.tensor_copy(Vh[:, :, 0:DH], V[:, :, bass.ds(h * DH, DH)]).then_inc(v_ready, 1)

            def split_maxima(m):
                pool.wait_ge(mx_chunk, m + 1)
                ch.step(nc.gpsimd.tensor_tensor(m_parts[:, 0, :], neg_m[:, :], zeros[:, :], ALU.add))
                ch.step(nc.gpsimd.tensor_tensor(m_rest[:, :], neg_m[:, :], m_parts[:, 0, :], ALU.subtract))
                ch.step(nc.gpsimd.tensor_tensor(m_parts[:, 1, :], m_rest[:, :], zeros[:, :], ALU.add))
                ch.step(nc.gpsimd.tensor_tensor(m_rest[:, :], m_rest[:, :], m_parts[:, 1, :], ALU.subtract))
                nc.gpsimd.tensor_tensor(m_parts[:, 2, :], m_rest[:, :], zeros[:, :], ALU.add).then_inc(mp_ready, 1)

            pool.wait_ge(pa_dve, PA_DVE.n("V"))
            copy_values(0)
            split_maxima(0)
            start = ch.total() - 4
            with pool.Fori(1, C) as m:
                ch.at(start + 4 * m)
                pool.wait_ge(mt_ready, m)
                split_maxima(m)
            with pool.Fori(0, H - 1) as h:
                with pool.Fori(0, C) as c:
                    m = C * (h + 1) + c
                    ch.at(start + 4 * m)
                    pool.wait_ge(mt_ready, m)
                    split_maxima(m)
                pool.wait_ge(pv_done, (h + 1) * T)
                copy_values(h + 1)

            pool_total = start + 4 * C * H
            pool.wait_ge(zero_out, 16 * (NT // FILL))
            pool.wait_ge(pos_set, 1)
            for t in range(T):
                for k in range(2):
                    pool.indirect_dma_start(xg_dram[:, :], bass.IndirectOffsetOnAxis(ap=pos_i[:, k, t:t + 1], axis=0),
                                            xn_rows[:, t, :], None).then_inc(scattered, 16)
            def scatter_outputs(b, half):
                pool.wait_ge(y_norm, b + 1)
                ch.did(pool.nop())
                for k in range(4 * half, 4 * half + 4):
                    pool.indirect_dma_start(yt_dram[:, :], bass.IndirectOffsetOnAxis(ap=dest[:, k:k + 1], axis=0),
                                            y_ring[:, k, :], None).then_inc(y_out, 16)

            scatter_outputs(0, 0)
            scatter_outputs(1, 1)
            with pool.Fori(1, NT // LOOP) as b:
                for half in range(2):
                    scatter_outputs(2 * b + half, half)
            pool.wait_ge(pool_chain, pool_total + NT // 4)

        @block.scalar
        def _(act):
            act.dma_start(ident, mats[:, 0:P]).then_inc(ident_in, 16)
            act.dma_start(mat_sb[:, P:MATS_1], mats[:, P:MATS_1]).then_inc(mats_in, 16)
            act.dma_start(col_sb[:, :], cols[:, :]).then_inc(cols_in, 16)
            act.dma_start(row_sb[:, :], rows.partition_broadcast(P)).then_inc(rows_in, 16)
            for c in range(C):
                act.wait_ge(ln_var, c + 1)
                nc.scalar.activation(rstd[:, c * TC:(c + 1) * TC], rstd[:, c * TC:(c + 1) * TC], ACT.Sqrt)\
                    .then_inc(ln_std, 1)
            act.wait_ge(ident_in, 16)
            nc.scalar.copy(ident_bf[:, :], ident).then_inc(identb_set, 1)
            for c in range(C):
                n = PA_MM.n("T", c)
                act.wait_ge(pa_mm, n)
                nc.scalar.copy(xnT[:, 1 + c * CH:1 + (c + 1) * CH], PS[:, bank_of(n), :]).then_inc(pa_act, 1)
            act.wait_ge(cols_in, 16)
            for c in range(C):
                n = PA_MM.n("X", c)
                act.wait_ge(pa_mm, n)
                nc.scalar.activation(xcT[:, c * CH:(c + 1) * CH], PS[:, bank_of(n), :], ACT.Identity,
                                     bias=col("conv_b")).then_inc(pa_act, 1)
            for step, full, parts, bias in (("Q", qf, qparts, "bq"), ("K", kf, kparts, "bk")):
                for c in range(C):
                    at = slice(c * CH, (c + 1) * CH)
                    n = PA_MM.n(step, c)
                    act.wait_ge(pa_mm, n)
                    nc.scalar.activation(full[:, at], PS[:, bank_of(n), :], ACT.Identity, bias=col(bias))\
                        .then_inc(full_set, 1)
                    nc.scalar.activation(parts[:, 0, at], PS[:, bank_of(n), :], ACT.Identity, bias=col(bias))\
                        .then_inc(pa_act, 1)
            for c in range(C):
                at = slice(c * CH, (c + 1) * CH)
                n = PA_MM.n("GD", 2 * c)
                act.wait_ge(pa_mm, n)
                nc.scalar.activation(sT[:, at], PS[:, bank_of(n), :], ACT.Relu).then_inc(gru_sig, 1)
                nc.scalar.activation(sig_h[:, at], PS[:, bank_of(n), :], ACT.Sigmoid).then_inc(pa_act, 1)
                n = PA_MM.n("GD", 2 * c + 1)
                act.wait_ge(pa_mm, n)
                nc.scalar.activation(gate_z[:, at], PS[:, bank_of(n), :], ACT.Sigmoid).then_inc(gru_sig, 1)
                nc.scalar.activation(gate_c[:, at], PS[:, bank_of(n), :], ACT.Sigmoid, scale=-1.0).then_inc(pa_act, 1)

            def copy_maxima(m):
                act.wait_ge(mt_ready, m + 1)
                if not (isinstance(m, int) and m == 0):
                    act.wait_ge(m_rows, 16 * m)
                nc.scalar.copy(mT[:, :], PS[0:PARTS * TC, MISC, 0:P // 2].bitcast(BF16)).then_inc(mt_copied, 1)

            def exps(h, k):
                if not (isinstance(h, int) and h == 0 and k < 2):
                    act.wait_ge(pv_done, h * T + k - 1)
                for i in range(C):
                    act.wait_ge(s_ready, (h * T + k) * C + i + 1)
                    nc.scalar.activation(probs[:, C * (k % 2) + i, :], PS[:, scores_bank(h, i), :], ACT.Exp,
                                         scale=DH ** -0.5).then_inc(exp_done, 1)

            def copy_output(h):
                act.wait_ge(pv_done, (h + 1) * T)
                if not (isinstance(h, int) and h == 0):
                    act.wait_ge(ot_ready, h)
                nc.scalar.copy(o_sum[:, :], PS[:, PVB, :]).then_inc(o_copied, 1)

            def head(h, output, maxima):
                for k in range(T):
                    exps(h, k)
                    if k == 0 and output:
                        copy_output(h - 1)
                    if k % 4 == 2 and maxima:
                        copy_maxima(C * (h + 1) + k // 4)

            for m in range(C):
                copy_maxima(m)
            head(0, False, True)
            with act.Fori(1, H - 1) as h:
                head(h, True, True)
            head(H - 1, True, False)
            copy_output(H - 1)

            for c in range(C):
                act.wait_ge(c_mm, C_MM.n("U", c))
                nc.scalar.copy(ctxT[:, c * CH:(c + 1) * CH], PS[:, bank_of(C_MM.n("U", c)), :]).then_inc(c_act, 1)
            for c in range(C):
                act.wait_ge(ln_var, C + c + 1)
                nc.scalar.activation(rstd[:, c * TC:(c + 1) * TC], rstd[:, c * TC:(c + 1) * TC], ACT.Sqrt)\
                    .then_inc(ln_std, 1)
            for c in range(C):
                act.wait_ge(c_mm, C_MM.n("Y", c))
                nc.scalar.activation(x1T[:, c * CH:(c + 1) * CH], PS[:, bank_of(C_MM.n("Y", c)), :], ACT.Identity,
                                     bias=col("ln1_b"), scale=col("ln1_g")).then_inc(c_act, 1)
            act.wait_ge(probs_exp, 1)
            nc.scalar.activation(gate_p[:, :, :], gate_p[:, :, :], ACT.Exp).then_inc(probs_exp, 1)
            for c in range(C):
                act.wait_ge(c_mm, C_MM.n("p", c))
                nc.scalar.copy(pT[:, c * CH:(c + 1) * CH], PS[0:E0, bank_of(C_MM.n("p", c)), :]).then_inc(c_act, 1)
            for c in range(2):
                act.wait_ge(c_mm, C_MM.n("s", c))
                nc.scalar.copy(p_stack[:, c * 2 * CH:(c + 1) * 2 * CH],
                               PS[0:PARTS * PICK, bank_of(C_MM.n("s", c)), :].bitcast(BF16)).then_inc(c_act, 1)

            def rectify(e, c, f):
                unit = (e * C + c) * FT + f
                act.wait_ge(h_mm, unit + 1)
                if not (isinstance(e, int) and unit < 2):
                    act.wait_ge(h_dve, unit - 1)
                act.nop().then_inc(bias_seen, 1)
                nc.scalar.activation(h_relu[:, f % 2, :], PS[:, HB + f % 2, :], ACT.Relu,
                                     bias=col_sb[:, bass.ds(COLS["b1"][0] + e * FT + f, 1)]).then_inc(h_act, 1)

            for c in range(C):
                for f in range(FT):
                    rectify(0, c, f)
            with act.Fori(1, E0 - 1) as e:
                for c in range(C):
                    for f in range(FT):
                        rectify(e, c, f)

            def copy_sum(c):
                n = E_MM.n("R", c)
                act.wait_ge(e_mm, n)
                nc.scalar.copy(x1[:, c * TC:(c + 1) * TC, :], PS[:, bank_of(n), :].rearrange("p (t d) -> p t d", t=TC))\
                    .then_inc(e_act, 1)

            def root(c):
                act.wait_ge(ln_var, 2 * C + c + 1)
                nc.scalar.activation(rstd[:, c * TC:(c + 1) * TC], rstd[:, c * TC:(c + 1) * TC], ACT.Sqrt)\
                    .then_inc(ln_std, 1)

            for c in range(C):
                for f in range(FT):
                    rectify(E0 - 1, c, f)
                    if c >= 2 and f == 1:
                        copy_sum(c - 2)
                    if c >= 2 and f == 3:
                        root(c - 2)
            act.wait_ge(bias_seen, E0 * C * FT)
            for c in range(C - 2, C):
                copy_sum(c)
            for c in range(C - 2, C):
                root(c)
            for c in range(C):
                act.wait_ge(norm2, c + 1)
                nc.scalar.activation(x1[:, c * TC:(c + 1) * TC, :], x1[:, c * TC:(c + 1) * TC, :], ACT.Silu)\
                    .then_inc(silu0, 1)

            for c in range(C):
                at = slice(c * TC, (c + 1) * TC)
                act.wait_ge(ln_var, 3 * C + c + 1)
                nc.scalar.activation(rstd[:, at], rstd[:, at], ACT.Sqrt).then_inc(ln_std, 1)
            act.wait_ge(rms_sum, 1)
            nc.scalar.activation(rms[:, :], rms[:, :], ACT.Sqrt).then_inc(rms_root, 1)
            for c in range(C):
                act.wait_ge(d_mm, D_MM.n("A", c))
                nc.scalar.copy(xn2T[:, c * CH:(c + 1) * CH], PS[:, bank_of(D_MM.n("A", c)), :]).then_inc(d_act, 1)
            act.wait_ge(rms_inv, 1)
            act.wait_ge(norm3, T)
            for t in range(T):
                nc.scalar.activation(hN[:, t, :], xn2[:, t, :], ACT.Copy, scale=rms[:, t:t + 1]).then_inc(h_norm, 1)
            act.wait_ge(route_exp, 1)
            nc.scalar.activation(rp[:, :, :], rp[:, :, :], ACT.Exp).then_inc(route_exp, 1)
            for c in range(C):
                act.wait_ge(d_mm, D_MM.n("B", c))
                nc.scalar.activation(hT[:, c * CH:(c + 1) * CH], PS[:, bank_of(D_MM.n("B", c)), :], ACT.Copy,
                                     scale=col("w_norm")).then_inc(d_act, 1)
            for j in range(2):
                for c in range(C):
                    n = D_MM.n("U", j * C + c)
                    act.wait_ge(d_mm, n)
                    nc.scalar.activation(u[j][:, c * CH:(c + 1) * CH], PS[:, bank_of(n), :], ACT.Silu)\
                        .then_inc(d_act, 1)
            for j in range(2):
                for c in range(C):
                    n = D_MM.n("M", j * C + c)
                    act.wait_ge(d_mm, n)
                    if j:
                        act.wait_ge(te_set, 1)
                    nc.scalar.activation(lam[j][:, c * CH:(c + 1) * CH], PS[:, bank_of(n), :], ACT.Sigmoid,
                                         bias=col("b_dt", j)).then_inc(d_act, 1)
            act.wait_ge(pos_set, 1)
            act.wait_ge(hot_w_set, 2)
            for j in range(2):
                for c in range(C):
                    n = D_MM.n("Z", j * C + c)
                    act.wait_ge(d_mm, n)
                    if j:
                        act.wait_ge(z_used, c + 1)
                    nc.scalar.activation(z_tmp[c], PS[:, bank_of(n), :], ACT.Silu).then_inc(d_act, 1)

            def copy_slots(n, k):
                act.wait_ge(xt_mm, n + 1)
                if not (isinstance(n, int) and n < 4):
                    act.wait_ge(g_mm, n - 3)
                nc.scalar.copy(xtT[:, k % 4, :], PS[:, XB, 0:P]).then_inc(xt_act, 1)

            def gate_slots(n, k):
                act.wait_ge(g_mm, n + 1)
                if not (isinstance(n, int) and n < 2):
                    act.wait_ge(gt_mm, n - 1)
                nc.scalar.activation(hid[:, k % 2, :], PS[:, H1B + k % 2, :], ACT.Silu).then_inc(g_act, 1)

            def copy_hidden(n, k):
                act.wait_ge(gt_mm, n + 1)
                if not (isinstance(n, int) and n < 2):
                    act.wait_ge(yt_mm, n - 1)
                nc.scalar.copy(hidT[:, k % 2, :], PS[:, GB, :]).then_inc(gt_act, 1)

            def roots(b, half):
                act.wait_ge(y_var, b + 1)
                at = slice(4 * half, 4 * half + 4)
                nc.scalar.activation(y_rstd[:, at], y_rstd[:, at], ACT.Sqrt).then_inc(y_std, 1)

            def experts_act(b, first, last):
                for k in range(LOOP):
                    n = LOOP * b + k
                    if not (last and k == LOOP - 1):
                        gate_slots(n + 1, k + 1)
                    copy_hidden(n, k)
                    if not (last and k >= LOOP - 3):
                        copy_slots(n + 3, k + 3)
                    if k == 1 and not first:
                        roots(2 * b - 1, 1)
                    if k == 5:
                        roots(2 * b, 0)

            d_free(act)
            copy_slots(0, 0)
            copy_slots(1, 1)
            copy_slots(2, 2)
            gate_slots(0, 0)
            experts_act(0, True, False)
            with act.Fori(1, NT // LOOP - 1) as b:
                experts_act(b, False, False)
            experts_act(NT // LOOP - 1, False, True)
            roots(NT // 4 - 1, 1)
            for c in range(C):
                act.wait_ge(hot_mm, c + 1)
                nc.scalar.copy(hot_wT[:, c * CH:(c + 1) * CH], PS[0:2 * E1, c, :]).then_inc(hot_act, 1)
            act.wait_ge(yt_mm, NT)
            act.wait_ge(g_mm, NT)
            for c in range(C):
                act.wait_ge(shift_mm, c + 1)
                nc.scalar.copy(chunk_shift(c), PS[:, C + c, :].rearrange("p (t d) -> p t d", t=TC)).then_inc(shift_act, 1)
            for c in range(C):
                act.wait_ge(mixed, c + 1)
                nc.scalar.activation(y1[:, c * TC:(c + 1) * TC, :], y1[:, c * TC:(c + 1) * TC, :], ACT.Silu)\
                    .then_inc(silu1, 1)

        @block.vector
        def _(dve):
            ch = Chain(dve, dve_chain)
            v = nc.vector

            def norm_stats(buf, c):
                for t in range(c * TC, (c + 1) * TC):
                    ch.did(v.bn_stats(stats[:, t, :], buf[:, t, :]))
                ch.settle()
                for t in range(c * TC, (c + 1) * TC):
                    ch.did(v.bn_aggr(moments[:, t, :], stats[:, t, :]))
                ch.settle()
                v.tensor_scalar(rstd[:, c * TC:(c + 1) * TC], moments[:, c * TC:(c + 1) * TC, 1], EPS, None,
                                ALU.add).then_inc(ln_var, 1)

            def norm_apply(out_buf, buf, c, calls, tile_done):
                dve.wait_ge(ln_std, C * calls + c + 1)
                ch.step(v.reciprocal(rstd[:, c * TC:(c + 1) * TC], rstd[:, c * TC:(c + 1) * TC]))
                for t in range(c * TC, (c + 1) * TC):
                    v.tensor_scalar(out_buf[:, t, :], buf[:, t, :], moments[:, t, 0:1], rstd[:, t:t + 1],
                                    ALU.subtract, ALU.mult).then_inc(tile_done, 1)

            for c in range(C + 1):
                if c < C:
                    dve.wait_ge(x_in[c], 16)
                    norm_stats(x_sb, c)
                if c > 0:
                    norm_apply(xn, x_sb, c - 1, 0, xn_ready)

            for i, (step, full, parts, ready) in enumerate((("Q", qf, qparts, split_q), ("K", kf, kparts, split_k))):
                for c in range(C):
                    at = slice(c * CH, (c + 1) * CH)
                    dve.wait_ge(full_set, i * C + c + 1)
                    dve.wait_ge(pa_act, PA_ACT.n(step, c))
                    ch.did(v.tensor_tensor(full[:, at], full[:, at], parts[:, 0, at], ALU.subtract))
                ch.settle()
                v.tensor_copy(parts[:, 1, :], full[:, :]).then_inc(ready, 1)
                dve.wait_ge(ready, 1)
                v.tensor_tensor(parts[:, 2, :], full[:, :], parts[:, 1, :], ALU.subtract).then_inc(ready, 1)
            dve.wait_ge(rows_in, 16)
            for c in range(C):
                n = PA_MM.n("V", c)
                dve.wait_ge(pa_mm, n)
                v.tensor_tensor(V[:, c * TC:(c + 1) * TC, :],
                                PS[:, bank_of(n), :].rearrange("p (t d) -> p t d", t=TC),
                                row("bv").unsqueeze(1).broadcast_to([P, TC, P]), ALU.add).then_inc(pa_dve, 1)
            for c in range(C):
                at = slice(c * CH, (c + 1) * CH)
                dve.wait_ge(gru_sig, 2 * (c + 1))
                dve.wait_ge(pa_act, PA_ACT.n("GD", 2 * c))
                ch.step(v.scalar_tensor_tensor(sT[:, at], sig_h[:, at], 0.5, sT[:, at], ALU.min, ALU.add))
                ch.step(v.tensor_tensor(sT[:, at], sT[:, at], gate_z[:, at], ALU.mult))
            dve.wait_ge(pa_act, PA_ACT.total)
            ch.did(v.tensor_tensor_scan(sT[:, :], gate_c[:, :], sT[:, :], 0.0, ALU.mult, ALU.add))

            def maxima(m, c, upto=TC, since=0):
                for j in range(since, upto):
                    if j == 0 and not (isinstance(m, int) and m < 2):
                        dve.wait_ge(mx_chunk, m - 1)
                    for half in range(2):
                        dve.wait_ge(mx_ready, 8 * m + 2 * j + half + 1)
                        v.tensor_reduce(mx[:, c % 2, 2 * j + half:2 * j + half + 1],
                                        PS[:, MB + 2 * half:MB + 2 * half + 2, :].rearrange("p b n -> p (b n)"),
                                        AX.X, ALU.max).then_inc(mx_used, 1)
                if upto == TC:
                    dve.wait_ge(mx_used, 8 * (m + 1))
                    if not (isinstance(m, int) and m == 0):
                        dve.wait_ge(mp_ready, m)
                    v.tensor_reduce(neg_m[:, :], mx[:, c % 2, :].rearrange("p (t b) -> p t b", b=2),
                                    AX.X, ALU.max, negate=True).then_inc(mx_chunk, 1)

            def normalise(h):
                dve.wait_ge(ot_ready, h + 1)
                o = PS[:, MISC, :].rearrange("p (i c w) -> p i c w", i=TC, c=C)
                inv = o_inv[:, :].rearrange("p (i c) -> p i c", i=TC)
                ch.step(v.reciprocal(inv, o[:, :, :, DH]))
                v.tensor_tensor(ctx_sb[:, :, bass.ds(h * DH, DH)].rearrange("p (c i) d -> p i c d", c=C),
                                o[:, :, :, 0:DH], inv.unsqueeze(3).broadcast_to([P, TC, C, DH]),
                                ALU.mult).then_inc(o_used, 1)

            for m in range(C + 1):
                maxima(m, m % C)
            dve.wait_ge(zero_out, 16 * (NT // FILL))
            for c in range(C):
                maxima(C + 1 + c, (c + 1) % C)
            start = ch.total() - 1
            with dve.Fori(1, H - 2) as h:
                ch.at(start + h)
                m = C * h + C + 1
                maxima(m, 1)
                maxima(m + 1, 2, upto=2)
                normalise(h - 1)
                maxima(m + 1, 2, since=2)
                maxima(m + 2, 3)
                maxima(m + 3, 0)
            ch.at(start + H - 2)
            m = C * (H - 1) + 1
            maxima(m, 1)
            maxima(m + 1, 2, upto=2)
            normalise(H - 3)
            maxima(m + 1, 2, since=2)
            maxima(m + 2, 3)
            normalise(H - 2)
            normalise(H - 1)

            def chunk(buf, c):
                return buf[:, c * TC:(c + 1) * TC, :]

            def bc(name, k=P):
                return row(name).unsqueeze(1).broadcast_to([P, TC, k])

            for c in range(C + 1):
                if c < C:
                    n = C_MM.n("O", c)
                    dve.wait_ge(c_mm, n)
                    v.tensor_tensor(chunk(x1, c), PS[:, bank_of(n), :].rearrange("p (t d) -> p t d", t=TC),
                                    bc("bo"), ALU.add).then_inc(c_dve, 1)
                    dve.wait_ge(c_dve, C_DVE.n("O", c))
                    norm_stats(x1, c)
                if c > 0:
                    norm_apply(x1, x1, c - 1, 1, ln1_done)
            dve.wait_ge(c_mm, C_MM.n("G"))
            v.tensor_tensor(gate_p[:, :, :], PS[:, bank_of(C_MM.n("G")), 0:T * E0].rearrange("p (t e) -> p t e", e=E0),
                            row("gate_b").unsqueeze(1).broadcast_to([P, T, E0]), ALU.add).then_inc(c_dve, 1)
            dve.wait_ge(c_dve, C_DVE.n("G"))
            ch.step(v.tensor_reduce(gate_s[:, :], gate_p[:, :, :], AX.X, ALU.max))
            v.tensor_tensor(gate_p[:, :, :], gate_p[:, :, :], gate_s[:, :].unsqueeze(2).broadcast_to([P, T, E0]),
                            ALU.subtract).then_inc(probs_exp, 1)
            dve.wait_ge(probs_exp, 2)
            ch.step(v.tensor_reduce(gate_s[:, :], gate_p[:, :, :], AX.X, ALU.add))
            ch.step(v.reciprocal(gate_s[:, :], gate_s[:, :]))
            v.tensor_tensor(gate_p[:, :, :], gate_p[:, :, :], gate_s[:, :].unsqueeze(2).broadcast_to([P, T, E0]),
                            ALU.mult).then_inc(pp_ready, 1)
            dve.wait_ge(pp_ready, 1)
            dve.wait_ge(consts_set, 2)
            for p in range(PARTS):
                part = gate_parts[:, :, p * PICK:p * PICK + E0]
                rest = gate_p if p == 0 else gate_rest
                ch.step(v.tensor_copy(part, rest[:, :, :]))
                if p < PARTS - 1:
                    ch.step(v.tensor_tensor(gate_rest[:, :, :], rest[:, :, :], part, ALU.subtract))
            dve.nop().then_inc(pp_ready, 1)

            def weigh(e, c, f):
                unit = (e * C + c) * FT + f
                if f == 0:
                    dve.wait_ge(p_mm, e * C + c + 1)
                dve.wait_ge(h_act, unit + 1)
                if not (isinstance(e, int) and unit < 4):
                    dve.wait_ge(y_mm, unit - 3)
                v.tensor_tensor(h_wt[:, f, :], h_relu[:, f % 2, :], PS[:, PB + c % 2, :], ALU.mult)\
                    .then_inc(h_dve, 1)

            for c in range(C):
                for f in range(FT):
                    weigh(0, c, f)
            with dve.Fori(1, E0 - 1) as e:
                for c in range(C):
                    for f in range(FT):
                        weigh(e, c, f)

            def add_residual(c):
                dve.wait_ge(y_mm, ((E0 - 1) * C + c + 1) * FT)
                v.tensor_tensor(ctxT[:, c * CH:(c + 1) * CH], PS[:, c, :], x1T[:, c * CH:(c + 1) * CH], ALU.add)\
                    .then_inc(r_dve, 1)

            def sum_stats(c):
                dve.wait_ge(e_act, c + 1)
                norm_stats(x1, c)

            def gain_shift(c):
                dve.wait_ge(norm2_tiles, (c + 1) * TC)
                ch.step(v.tensor_tensor(chunk(x1, c), chunk(x1, c), bc("ln2_g"), ALU.mult))
                v.tensor_tensor(chunk(x1, c), chunk(x1, c), bc("ln2_b"), ALU.add).then_inc(norm2, 1)

            for c in range(C):
                for f in range(FT):
                    weigh(E0 - 1, c, f)
                    if c >= 1 and f == 1:
                        add_residual(c - 1)
                    if c >= 2 and f == 2:
                        sum_stats(c - 2)
                    if c >= 2 and f == 3:
                        norm_apply(x1, x1, c - 2, 2, norm2_tiles)
                    if c >= 3 and f == 0:
                        gain_shift(c - 3)
            add_residual(C - 1)
            gain_shift(C - 3)
            sum_stats(C - 2)
            sum_stats(C - 1)
            for c in range(C - 2, C):
                norm_apply(x1, x1, c, 2, norm2_tiles)
                gain_shift(c)
            for c in range(C):
                dve.wait_ge(silu0, c + 1)
                n = E_MM.n("S", c)
                dve.wait_ge(e_mm, n)
                v.tensor_tensor(chunk(x1, c), chunk(x1, c),
                                PS[:, bank_of(n), :].rearrange("p (t d) -> p t d", t=TC),
                                ALU.mult).then_inc(e_dve, 1)
                dve.wait_ge(e_dve, c + 1)
                v.tensor_tensor(chunk(x_sb, c), chunk(x_sb, c), chunk(x1, c), ALU.add).then_inc(x_ready, 1)
                dve.wait_ge(x_ready, c + 1)
                norm_stats(x_sb, c)
                if c > 0:
                    norm_apply(xn2, x_sb, c - 1, 3, norm3)
            norm_apply(xn2, x_sb, C - 1, 3, norm3)
            ch.step(v.tensor_tensor(rms[:, :], moments[:, :, 1], rstd[:, :], ALU.mult))
            ch.step(v.tensor_tensor(rms[:, :], rms[:, :], rstd[:, :], ALU.mult))
            v.tensor_scalar(rms[:, :], rms[:, :], EPS, None, ALU.add).then_inc(rms_sum, 1)
            dve.wait_ge(rms_root, 1)
            v.reciprocal(rms[:, :], rms[:, :]).then_inc(rms_inv, 1)

            def over_e(a):
                return a.unsqueeze(2).broadcast_to([P, T, E1])

            dve.wait_ge(d_mm, D_MM.n("L"))
            v.tensor_tensor(rp[:, :, :], PS[:, bank_of(D_MM.n("L")), 0:T * E1].rearrange("p (t e) -> p t e", e=E1),
                            row("br").unsqueeze(1).broadcast_to([P, T, E1]), ALU.add).then_inc(d_dve, 1)
            dve.wait_ge(d_dve, D_DVE.n("L"))
            ch.step(v.tensor_reduce(rs[:, :], rp[:, :, :], AX.X, ALU.max))
            v.tensor_tensor(rp[:, :, :], rp[:, :, :], over_e(rs[:, :]), ALU.subtract).then_inc(route_exp, 1)
            dve.wait_ge(route_exp, 2)
            ch.step(v.tensor_reduce(rs[:, :], rp[:, :, :], AX.X, ALU.add))
            ch.step(v.reciprocal(rs[:, :], rs[:, :]))
            ch.step(v.tensor_tensor(rp[:, :, :], rp[:, :, :], over_e(rs[:, :]), ALU.mult))
            for t in range(T):
                ch.did(v.max(top[:, t, :], rp[:, t, :]))
            ch.settle()
            for t in range(T):
                ch.did(v.max_index(top_i[:, t, :], top[:, t, :], rp[:, t, :]))
            ch.did(v.tensor_tensor(rs[:, :], top[:, :, 0], top[:, :, 1], ALU.add))
            ch.settle()
            ch.did(v.tensor_copy(top_f[:, :, :], top_i[:, :, 0:2].rearrange("p t k -> p k t")))
            ch.did(v.reciprocal(rs[:, :], rs[:, :]))
            ch.settle()
            for k in range(2):
                ch.did(v.tensor_tensor(wgt[:, k, :], top[:, :, k], rs[:, :], ALU.mult))
                ch.did(v.tensor_tensor(hot[:, k, :, :], row("iota")[:, 0:E1].unsqueeze(1).broadcast_to([P, T, E1]),
                                       over_e(top_f[:, k, :]), ALU.is_equal))
            ch.settle()
            v.tensor_tensor(mask[:, :, :], hot[:, 0, :, :], hot[:, 1, :, :], ALU.add).then_inc(mask_set, 1)

            n = D_MM.n("K")
            dve.wait_ge(d_mm, n)
            kb = PS[:, bank_of(n), :].rearrange("p (a t e) -> p a t e", a=2, t=T)
            ch.step(v.tensor_copy(tot[:, :, :], kb[:, 1, :, :].rearrange("p t e -> p e t")))
            ch.step(v.tensor_tensor_scan(upto[:, :, :].rearrange("p e t -> p (e t)"),
                                         reset[:, :, :].rearrange("p e t -> p (e t)"),
                                         tot[:, :, :].rearrange("p e t -> p (e t)"), 0.0, ALU.mult, ALU.add))
            ch.step(v.tensor_scalar(te_thr[:, :], row("iota")[:, 0:T], float(P), None, ALU.mult))
            ch.step(v.tensor_tensor(place[:, :, :].rearrange("p t e -> p (t e)").rearrange("p (e t) -> p e t", e=E1),
                                    upto[:, :, T - 1:T].broadcast_to([P, E1, T]),
                                    te_thr[:, :].unsqueeze(1).broadcast_to([P, E1, T]), ALU.is_gt))
            ch.step(v.tensor_reduce(n_tiles[:, :], place[:, :, :].rearrange("p t e -> p (t e)").rearrange("p (e t) -> p e t", e=E1), AX.X, ALU.add))
            ch.step(v.tensor_tensor_scan(end[:, :], reset[:, 0, 1:2].broadcast_to([P, E1]), n_tiles[:, :], 0.0,
                                         ALU.mult, ALU.add))
            ch.step(v.tensor_tensor(upto[:, :, :], upto[:, :, :], tot[:, :, :], ALU.subtract))
            ch.step(v.tensor_tensor(n_tiles[:, :], end[:, :], n_tiles[:, :], ALU.subtract))
            ch.step(v.scalar_tensor_tensor(upto[:, :, :], n_tiles[:, :].unsqueeze(2).broadcast_to([P, E1, T]), float(P),
                                           upto[:, :, :], ALU.mult, ALU.add))
            v.tensor_tensor(place[:, :, :], upto[:, :, :].rearrange("p e t -> p t e"), kb[:, 0, :, :],
                            ALU.add).then_inc(d_dve, 1)
            dve.wait_ge(d_dve, D_DVE.n("K"))
            for k in range(2):
                ch.step(v.tensor_tensor(rp[:, :, :], hot[:, k, :, :], place[:, :, :], ALU.mult))
                ch.step(v.tensor_reduce(pos[:, k, :], rp[:, :, :], AX.X, ALU.add))
            dve.wait_ge(cols_in, 16)
            ch.did(v.tensor_copy(xn_rows[:, :, P:P + 1], col_sb[:, COLS["token"][0]:COLS["token"][1]].unsqueeze(2)))
            ch.did(v.tensor_copy(xn_rows[:, :, P + 1:P + 2], top_f[:, 0, :].unsqueeze(2)))
            ch.settle()
            v.tensor_copy(pos_i[:, :, :], pos[:, :, :]).then_inc(pos_set, 1)
            for k in range(2):
                v.tensor_tensor(hot_w[:, :, k * E1:(k + 1) * E1], hot[:, k, :, :], over_e(wgt[:, k, :]), ALU.mult)\
                    .then_inc(hot_w_set, 1)
            dve.wait_ge(d_act, D_ACT.n("B"))
            dve.wait_ge(d_mm, D_MM.n("B"))
            ch.step(v.tensor_tensor(te_cmp, row("iota").unsqueeze(2).broadcast_to([P, NT, E1]),
                                    end[:, :].unsqueeze(1).broadcast_to([P, NT, E1]), ALU.is_ge))
            ch.step(v.tensor_reduce(te[:, :], te_cmp, AX.X, ALU.add))
            ch.step(v.tensor_scalar(te[:, :], te[:, :], float(E1 - 1), None, ALU.min))
            v.tensor_copy(te_i[:, :], te[0:1, :]).then_inc(te_set, 1)

            dve.wait_ge(d_act, D_ACT.n("M"))
            for j in range(2):
                ch.step(v.scalar_tensor_tensor(u[j][:, :], lam[j][:, :], 1.0, u[j][:, :], ALU.subtract, ALU.mult))
                ch.step(v.tensor_tensor_scan(lam[j][:, :], lam[j][:, :], u[j][:, :], 0.0, ALU.mult, ALU.subtract))
            for j in range(2):
                for c in range(C):
                    dve.wait_ge(d_act, D_ACT.n("Z", j * C + c))
                    v.tensor_tensor(lam[j][:, c * CH:(c + 1) * CH], lam[j][:, c * CH:(c + 1) * CH], z_tmp[c],
                                    ALU.mult).then_inc(z_used, 1)
            for c in range(C):
                n = D_MM.n("Y", c)
                dve.wait_ge(d_mm, n)
                v.tensor_tensor(chunk(s1, c), PS[:, bank_of(n), :].rearrange("p (t d) -> p t d", t=TC),
                                chunk(xn2, c), ALU.add).then_inc(d_dve, 1)
            dve.wait_ge(d_dve, D_DVE.n("Y"))
            dve.nop().then_inc(s_gated, C)

            def multiply(n, k):
                dve.wait_ge(g_act, n + 1)
                v.tensor_tensor(hid[:, k % 2, :], hid[:, k % 2, :], PS[:, H3B + k % 2, :], ALU.mult).then_inc(g_dve, 1)

            def find_rows(n, k, loads):
                dve.wait_ge(xt_in[k % 4], 16 * loads)
                v.tensor_scalar(other[:, k % 4:k % 4 + 1], xt[:, k % 4, P + 1:P + 2], te[:, bass.ds(n, 1)], float(N),
                                ALU.not_equal, ALU.mult).then_inc(other_set, 1)
                dve.wait_ge(other_set, n + 1)
                v.tensor_tensor(dest_f[:, bass.ds(n, 1)], xt[:, k % 4, P:P + 1], other[:, k % 4:k % 4 + 1], ALU.add)\
                    .then_inc(dest_set, 1)

            def take_output(n, k):
                dve.wait_ge(yt_mm, n + 1)
                if k % 4 == 0 and not (isinstance(n, int) and n < LOOP):
                    dve.wait_ge(y_out, 16 * n - 64)
                v.tensor_copy(y_ring[:, k, :], PS[:, YB + k % 2, 0:P]).then_inc(yt_dve, 1)
                dve.wait_ge(yt_dve, n + 1)
                ch.step(v.bn_stats(y_st[:, k, :], y_ring[:, k, :]))
                ch.did(dve.nop())
                ch.step(v.bn_aggr(y_mom[:, k, :], y_st[:, k, :]))
                if k % 4 == 3:
                    v.tensor_scalar(y_rstd[:, k - 3:k + 1], y_mom[:, k - 3:k + 1, 1], EPS, None, ALU.add)                        .then_inc(y_var, 1)

            def finish_outputs(b, half):
                dve.wait_ge(dest_set, 4 * b + 4)
                dve.wait_ge(y_std, b + 1)
                at = slice(4 * half, 4 * half + 4)
                ch.did(v.reciprocal(y_rstd[:, at], y_rstd[:, at]))
                ch.did(v.tensor_copy(dest[:, at], dest_f[:, bass.ds(4 * b, 4)]))
                ch.settle()
                for k in range(4 * half, 4 * half + 4):
                    ch.did(v.tensor_scalar(y_ring[:, k, :], y_ring[:, k, :], y_mom[:, k, 0:1], y_rstd[:, k:k + 1],
                                           ALU.subtract, ALU.mult))
                ch.settle()
                dve.nop().then_inc(y_norm, 1)

            def experts_dve(b, first, last):
                for k in range(LOOP):
                    n = LOOP * b + k
                    if not (last and k == LOOP - 1):
                        multiply(n + 1, k + 1)
                    if not (first and k == 0):
                        take_output(n - 1, (k - 1) % LOOP)
                    if not (last and k >= LOOP - 3):
                        find_rows(n + 3, k + 3, 2 * b + 1 + (k + 3) // 4)
                    if k == 2 and not first:
                        finish_outputs(2 * b - 1, 1)
                    if k == 6:
                        finish_outputs(2 * b, 0)

            dve.wait_ge(te_set, 1)
            for k in range(3):
                find_rows(k, k, 1)
            multiply(0, 0)
            experts_dve(0, True, False)
            per = LOOP * 3 + 2 * (2 + 4)
            start = ch.total()
            with dve.Fori(1, NT // LOOP - 1) as b:
                ch.at(start + (b - 1) * per)
                experts_dve(b, False, False)
                assert ch.n == per, ch.n
            ch.at(start + (NT // LOOP - 2) * per)
            experts_dve(NT // LOOP - 1, False, True)
            take_output(NT - 1, LOOP - 1)
            finish_outputs(NT // 4 - 1, 1)

            for c in range(C):
                dve.wait_ge(rows_back[c], 16 * 2)
                dve.wait_ge(gain_mm, (c + 1) * TC)
                dve.wait_ge(shift_act, c + 1)
                g1, g2 = (PS[:, 2 * c:2 * c + 2, :].rearrange("p b (i w) -> p (b i) w", i=2)[:, :, i * P:(i + 1) * P]
                          for i in range(2))
                ch.did(v.tensor_tensor(chunk(y1, c), chunk(y1, c), g1, ALU.mult))
                ch.did(v.tensor_tensor(chunk(y2, c), chunk(y2, c), g2, ALU.mult))
                ch.settle()
                ch.step(v.tensor_tensor(chunk(y1, c), chunk(y1, c), chunk(y2, c), ALU.add))
                v.tensor_tensor(chunk(y1, c), chunk(y1, c), chunk_shift(c), ALU.add).then_inc(mixed, 1)
            for c in range(C):
                dve.wait_ge(silu1, c + 1)
                ch.step(v.tensor_tensor(chunk(y1, c), chunk(y1, c), chunk(s1, c), ALU.mult))
                v.tensor_tensor(chunk(x_sb, c), chunk(x_sb, c), chunk(y1, c), ALU.add).then_inc(done, 1)

        @block.tensor
        def _(pe):
            pe.wait_ge(ident_in, 16)

            def transposes(c):
                def mms(bank):
                    for i in range(TC):
                        pe.wait_ge(xn_ready, c * TC + i + 1)
                        last = pe.transpose(bank[:, i * P:(i + 1) * P], xn[:, c * TC + i, :], ident)
                    return last
                return mms

            def conv(c):
                def mms(bank):
                    pe.wait_ge(pa_act, min(c + 2, C))
                    for k in range(3):
                        last = pe.matmul(bank, mat("conv")[:, k * P:(k + 1) * P], xnT[:, c * CH + k:c * CH + k + CH],
                                         start=(k == 0), stop=(k == 2))
                    return last
                return mms

            def project(weights, src):
                return lambda c: lambda bank: pe.matmul(bank, weights, src[:, c * CH:(c + 1) * CH],
                                                        start=True, stop=True)

            def values(c):
                def mms(bank):
                    for i in range(TC):
                        t = c * TC + i
                        last = pe.matmul(bank[:, i * P:(i + 1) * P], xcT[:, t * P:(t + 1) * P],
                                         mat("qkv")[:, 2 * P:3 * P], start=True, stop=True)
                    return last
                return mms

            def first(step, c, mms):
                mms(PS[:, bank_of(PA_MM.n(step, c)), :]).then_inc(pa_mm, 1)

            for c in range(C):
                first("T", c, transposes(c))
            pe.wait_ge(mats_in, 16)
            pe.wait_ge(edges_set, 2)
            for c in range(C):
                first("X", c, conv(c))
            for c in range(C):
                pe.wait_ge(pa_act, PA_ACT.n("X", c))
                first("Q", c, project(mat("qkv")[:, 0:P], xcT)(c))
            for c in range(C):
                first("K", c, project(mat("qkv")[:, P:2 * P], xcT)(c))
            for c in range(C):
                pe.wait_ge(pa_act, PA_ACT.n("Q", c))
                first("V", c, values(c))
            for c in range(2 * C):
                if c < C:
                    pe.wait_ge(pa_act, PA_ACT.n("K", c))
                else:
                    pe.wait_ge(pa_dve, PA_DVE.n("V", c - C))
                at = c % 2 * P
                first("GD", c, project(mat("gru")[:, at:at + P], xnT[:, 1:N + 1])(c // 2))

            def slot(h):
                return (h % RING) * N

            def maxima_tile(mh, k, i):
                unit = mh * T + k
                if i % 2 == 0 and not (isinstance(mh, int) and unit == 0):
                    pe.wait_ge(mx_used, 2 * unit + i // 2 - 1)
                mm = pe.matmul(PS[:, MB + i, :], q_ring[0:MROW, bass.ds(slot(mh) + k * P, P)],
                               k_ring[0:MROW, bass.ds(slot(mh) + i * CH, CH)], start=True, stop=True)
                if i % 2 == 1:
                    mm.then_inc(mx_ready, 1)

            def scores_tile(h, k, i):
                if isinstance(h, int) and h == H - 1 and k > 0:
                    pe.wait_ge(exp_done, (h * T + k - 1) * C + i + 1)
                elif isinstance(h, int) and h == H - 1 and i >= 2:
                    pe.wait_ge(mx_used, 2 * T * H)
                elif not (isinstance(h, int) and h == 0 and k == 0 and i < 2):
                    pe.wait_ge(exp_done, (h * T + k) * C + i - 1)
                pe.matmul(PS[:, scores_bank(h, i), :], k_ring[0:KS, bass.ds(slot(h) + k * P, P)],
                          q_ring[0:KS, bass.ds(slot(h) + i * CH, CH)], start=True, stop=True).then_inc(s_ready, 1)

            def weigh_values(h, k):
                pe.wait_ge(exp_done, (h * T + k) * C + C)
                if k == 0:
                    pe.wait_ge(v_ready, h + 1)
                    if not (isinstance(h, int) and h == 0):
                        pe.wait_ge(o_copied, h)
                for i in range(C):
                    mm = pe.matmul(PS[VW * i:VW * (i + 1), PVB, :], Vh[:, k, :], probs[:, C * (k % 2) + i, :],
                                   start=(k == 0), stop=(k == T - 1))
                mm.then_inc(pv_done, 1)

            def turn_maxima(m, outputs):
                pe.wait_ge(mp_ready, m + 1)
                if not (isinstance(m, int) and m == 0):
                    pe.wait_ge(mt_copied, m)
                if outputs is not None:
                    pe.wait_ge(o_used, outputs)
                pe.transpose(PS[0:PARTS * TC, MISC, 0:P // 2].bitcast(BF16),
                             m_parts[:, :, :].rearrange("p a t -> p (a t)"), ident_bf[:, :]).then_inc(mt_ready, 1)

            def turn_output(h, m):
                pe.wait_ge(o_copied, h + 1)
                if m is not None:
                    pe.wait_ge(mt_copied, m)
                for i in range(TC):
                    mm = pe.transpose(PS[:, MISC, i * P:(i + 1) * P], o_sum[:, i * P:(i + 1) * P], ident)
                mm.then_inc(ot_ready, 1)

            def pair(h, k, with_maxima):
                if k == 0:
                    pe.wait_ge(m_rows, 16 * C * (h + 1))
                mh, mk = h + (k + T + C) // T, (k + C) % T
                if with_maxima and mk == 0:
                    pe.wait_ge(heads_in, 96 * mh)
                for what, i in SCORES_ORDER:
                    if what == "scores":
                        scores_tile(h, k, i)
                    elif with_maxima:
                        maxima_tile(mh, mk, i)

            def head(h, first_head, last):
                for k in range(T):
                    if k < T - 1:
                        pair(h, k + 1, last > 1 or (last == 1 and k + 1 < T - C))
                    elif last > 0:
                        pair(h + 1, 0, last > 1)
                    if k % C == 1 and last > 0:
                        turn_maxima(C * (h + 1) + k // C, None if first_head else h - 1 if k < C else h)
                    weigh_values(h, k)
                    if k == C - 1 and not first_head:
                        turn_output(h - 1, C * (h + 1) + 1 if last > 0 else C * H)

            pe.wait_ge(pa_act, PA_ACT.total)
            pe.wait_ge(pa_dve, PA_DVE.total)
            pe.wait_ge(identb_set, 1)
            pe.wait_ge(head0_in, 96)
            for unit in range(T + C):
                if unit == T:
                    pe.wait_ge(heads_in, 96 * 2)
                for i in range(C):
                    maxima_tile(unit // T, unit % T, i)
                if unit % C == C - 1 and unit > C:
                    turn_maxima(unit // C - 1, None)
            pair(0, 0, True)
            head(0, True, H - 1)
            with pe.Fori(1, H - 2) as h:
                head(h, False, 2)
            head(H - 2, False, 1)
            head(H - 1, False, 0)
            pe.wait_ge(o_used, H - 1)
            turn_output(H - 1, None)
            pe.wait_ge(o_used, H)
            pe.wait_ge(mx_used, 8 * H * C)
            pe.wait_ge(mats2_in, 16)
            pe.wait_ge(small_in, 64)

            def fill(step, c, mms):
                mms(PS[:, bank_of(C_MM.n(step, c)), :]).then_inc(c_mm, 1)

            def turn_tiles(src, ready=None):
                def mms(bank):
                    for i in range(TC):
                        last = pe.transpose(bank[:, i * P:(i + 1) * P], src(i), ident)
                    return last
                return mms

            for c in range(C):
                fill("U", c, turn_tiles(lambda i: ctx_sb[:, c * TC + i, :]))
            for c in range(C):
                def mms(bank):
                    for i in range(TC):
                        at = slice((c * TC + i) * P, (c * TC + i + 1) * P)
                        pe.matmul(bank[:, i * P:(i + 1) * P], ctxT[:, at], mat("wo"), start=True, stop=False)
                        last = pe.matmul(bank[:, i * P:(i + 1) * P], xcT[:, at], ident, start=False, stop=True)
                    return last
                pe.wait_ge(c_act, C_ACT.n("U", c))
                fill("O", c, mms)
            def gate(c):
                pe.wait_ge(c_act, C_ACT.n("Y", c))
                for t in range(c * TC, (c + 1) * TC):
                    last = pe.matmul(PS[:, bank_of(C_MM.n("G")), t * E0:(t + 1) * E0], x1T[:, t * P:(t + 1) * P],
                                     mat("gate"), start=True, stop=True)
                return last

            pe.wait_ge(c_dve, C_DVE.n("O"))
            for c in range(C):
                pe.wait_ge(ln1_done, (c + 1) * TC)
                pe.wait_ge(c_act, C_ACT.n("U", c))
                fill("Y", c, turn_tiles(lambda i: x1[:, c * TC + i, :]))
                if c > 0:
                    gate(c - 1)
            gate(C - 1).then_inc(c_mm, 1)
            pe.wait_ge(pp_ready, 1)
            for c in range(C):
                def mms(bank):
                    for i in range(TC):
                        last = pe.transpose(bank[0:E0, i * P:(i + 1) * P], gate_p[:, c * TC + i, :], ident)
                    return last
                pe.wait_ge(c_dve, C_DVE.n("O"))
                fill("p", c, mms)
            pe.wait_ge(pp_ready, 2)
            for c in range(2):
                def mms(bank):
                    for i in range(2 * TC):
                        last = pe.transpose(bank[0:PARTS * PICK, i * P // 2:(i + 1) * P // 2].bitcast(BF16),
                                            gate_parts[:, c * 2 * TC + i, :], ident_bf[:, :])
                    return last
                fill("s", c, mms)

            pe.wait_ge(c_act, C_ACT.total)
            pe.wait_ge(c_dve, C_DVE.total)
            for c in range(C):
                pe.matmul(PS[:, c, :], b2_sb[:, :], pT[:, c * CH:(c + 1) * CH], start=True, stop=False)

            def spread(e, c):
                if not (isinstance(e, int) and e == 0 and c < 2):
                    pe.wait_ge(h_dve, (e * C + c - 1) * FT)
                pe.matmul(PS[:, PB + c % 2, :], pick_sb[:, bass.ds(e * P, P)], p_stack[:, c * CH:(c + 1) * CH],
                          start=True, stop=True).then_inc(p_mm, 1)

            def hidden(e, par, c, f, loads):
                unit = (e * C + c) * FT + f
                if c == 0 and f == 0:
                    pe.wait_ge(w1_in[par], 16 * loads)
                if f == 0:
                    spread(e, c)
                if not (isinstance(e, int) and unit < 2):
                    pe.wait_ge(h_act, unit - 1)
                pe.matmul(PS[:, HB + f % 2, :], w1_buf[:, par, f * P:(f + 1) * P], x1T[:, c * CH:(c + 1) * CH],
                          start=True, stop=True).then_inc(h_mm, 1)

            def add_up(e, par, c, f, loads, last):
                unit = (e * C + c) * FT + f
                if c == 0 and f == 0:
                    pe.wait_ge(w2_in[par], 16 * loads)
                pe.wait_ge(h_dve, unit + 1)
                pe.matmul(PS[:, c, :], w2_buf[:, par, f * P:(f + 1) * P], h_wt[:, f, :],
                          start=False, stop=last and f == FT - 1).then_inc(y_mm, 1)

            def fill(step, c, mms):
                mms(PS[:, bank_of(E_MM.n(step, c)), :]).then_inc(e_mm, 1)

            def turn_sum(c):
                pe.wait_ge(r_dve, c + 1)
                fill("R", c, turn_tiles(lambda i: ctxT[:, (c * TC + i) * P:(c * TC + i + 1) * P]))

            def experts(pair, final):
                per = C * FT
                for u in range(2 * per):
                    n = u + 2
                    if n < 2 * per:
                        hidden(2 * pair + n // per, n // per, n % per // FT, n % FT, pair + 1)
                    elif not final:
                        hidden(2 * pair + 2, 0, 0, n - 2 * per, pair + 2)
                    add_up(2 * pair + u // per, u // per, u % per // FT, u % FT, pair + 1,
                           final and u >= per)
                    if final and u >= per + FT and u % FT == FT - 1 and u < 2 * per - 1:
                        turn_sum(u % per // FT - 1)

            hidden(0, 0, 0, 0, 1)
            hidden(0, 0, 0, 1, 1)
            experts(0, False)
            with pe.Fori(1, E0 // 2 - 1) as pair_of:
                experts(pair_of, False)
            experts(E0 // 2 - 1, True)
            turn_sum(C - 2)
            turn_sum(C - 1)
            pe.wait_ge(h_dve, E0 * C * FT)
            for c in range(C):
                fill("S", c, turn_tiles(lambda i: sT[:, (c * TC + i) * P:(c * TC + i + 1) * P]))

            def fill(step, c, mms):
                mms(PS[:, bank_of(D_MM.n(step, c)), :]).then_inc(d_mm, 1)

            pe.wait_ge(e_act, C)
            pe.wait_ge(e_dve, C)
            def logits(c):
                pe.wait_ge(d_act, D_ACT.n("A", c))
                for t in range(c * TC, (c + 1) * TC):
                    last = pe.matmul(PS[:, bank_of(D_MM.n("L")), t * E1:(t + 1) * E1], xn2T[:, t * P:(t + 1) * P],
                                     mat("wr"), start=True, stop=True)
                return last

            for c in range(C):
                pe.wait_ge(norm3, (c + 1) * TC)
                fill("A", c, turn_tiles(lambda i: xn2[:, c * TC + i, :]))
                if c > 0:
                    logits(c - 1)
            logits(C - 1).then_inc(d_mm, 1)
            for c in range(C):
                pe.wait_ge(h_norm, (c + 1) * TC)
                fill("B", c, turn_tiles(lambda i: hN[:, c * TC + i, :]))

            def from_h(part, c):
                return lambda bank: pe.matmul(bank, mat("win")[:, part * P:(part + 1) * P],
                                              hT[:, c * CH:(c + 1) * CH], start=True, stop=True)
            for c in range(C):
                pe.wait_ge(d_act, D_ACT.n("B", c))
                if c == C - 1:
                    pe.wait_ge(d_dve, D_DVE.n("L"))
                fill("U", c, from_h(0, c))
            for c in range(C):
                fill("U", C + c, from_h(1, c))

            def count(bank):
                m = mask[:, :, :].rearrange("p t e -> p (t e)")
                pe.matmul(bank[:, 0:T * E1], tri_bf[:, 0:P], m, start=True, stop=True)
                return pe.matmul(bank[:, T * E1:2 * T * E1], tri_bf[:, P:2 * P], m, start=True, stop=True)
            pe.wait_ge(mask_set, 1)
            pe.wait_ge(d_act, D_ACT.n("U", 0))
            fill("K", 0, count)
            for j in range(2):
                for c in range(C):
                    def mms(bank):
                        for i in range(2):
                            at = (i * 2 + j) * P
                            last = pe.matmul(bank, mat("wdt")[:, at:at + P], u[i][:, c * CH:(c + 1) * CH],
                                             start=(i == 0), stop=(i == 1))
                        return last
                    i = j * C + c
                    if j == 0:
                        pe.wait_ge(d_act, D_ACT.n("U", C + c))
                    if i == 2 * C - 1:
                        pe.wait_ge(d_dve, D_DVE.n("K"))
                    fill("M", i, mms)
            for j in range(2):
                for c in range(C):
                    pe.wait_ge(d_act, D_ACT.n("M", j * C + c))
                    fill("Z", j * C + c, from_h(2 + j, c))
            for c in range(C):
                def mms(bank):
                    for i in range(TC):
                        at = slice((c * TC + i) * P, (c * TC + i + 1) * P)
                        for j in range(2):
                            last = pe.matmul(bank[:, i * P:(i + 1) * P], lam[j][:, at],
                                             mat("wout")[:, j * P:(j + 1) * P], start=(j == 0), stop=(j == 1))
                    return last
                pe.wait_ge(z_used, C + c + 1)
                pe.wait_ge(d_act, D_ACT.n("Z", c))
                fill("Y", c, mms)

            def expert(n):
                return pe.value_load(te_i[0:1, bass.ds(n, 1)], min_val=0, max_val=E1 - 1)

            def turn_slots(n, k, loads):
                pe.wait_ge(xt_in[k % 4], 16 * loads)
                if not (isinstance(n, int) and n == 0):
                    pe.wait_ge(xt_act, n)
                pe.transpose(PS[:, XB, 0:P], xt[:, k % 4, 0:P], ident).then_inc(xt_mm, 1)

            def hidden_slots(n, k):
                e = expert(n)
                pe.wait_ge(xt_act, n + 1)
                if not (isinstance(n, int) and n < 2):
                    pe.wait_ge(g_dve, n - 1)
                for b, w in ((H1B, 0), (H3B, F1)):
                    mm = pe.matmul(PS[:, b + k % 2, :], xtT[:, k % 4, :], big[:, bass.ds(e * W_ALL + w, F1)],
                                   start=True, stop=True)
                mm.then_inc(g_mm, 1)

            def turn_hidden(n, k):
                pe.wait_ge(g_dve, n + 1)
                if not (isinstance(n, int) and n == 0):
                    pe.wait_ge(gt_act, n)
                for f in range(F1 // P):
                    mm = pe.transpose(PS[:, GB, f * P:(f + 1) * P], hid[:, k % 2, f * P:(f + 1) * P], ident)
                mm.then_inc(gt_mm, 1)

            def outputs(n, k):
                e = expert(n)
                pe.wait_ge(gt_act, n + 1)
                if not (isinstance(n, int) and n < 2):
                    pe.wait_ge(yt_dve, n - 1)
                for f in range(F1 // P):
                    mm = pe.matmul(PS[:, YB + k % 2, 0:P], hidT[:, k % 2, f * P:(f + 1) * P],
                                   big[:, bass.ds(e * W_ALL + 2 * F1 + f * P, P)],
                                   start=(f == 0), stop=(f == F1 // P - 1))
                mm.then_inc(yt_mm, 1)

            def experts_pe(b, first, last):
                for k in range(LOOP):
                    n = LOOP * b + k
                    if not (last and k == LOOP - 1):
                        hidden_slots(n + 1, k + 1)
                    if not (first and k == 0):
                        outputs(n - 1, k + 1)
                    turn_hidden(n, k)
                    if not (last and k >= LOOP - 3):
                        turn_slots(n + 3, k + 3, 2 * b + 1 + (k + 3) // 4)

            pe.wait_ge(d_act, D_ACT.total)
            pe.wait_ge(d_dve, D_DVE.total)
            pe.wait_ge(te_set, 1)
            pe.wait_ge(wall_in, 64)
            turn_slots(0, 0, 1)
            turn_slots(1, 1, 1)
            turn_slots(2, 2, 1)
            hidden_slots(0, 0)
            experts_pe(0, True, False)
            with pe.Fori(1, NT // LOOP - 1) as b:
                experts_pe(b, False, False)
            experts_pe(NT // LOOP - 1, False, True)
            outputs(NT - 1, 1)

            pe.wait_ge(hot_w_set, 2)
            pe.wait_ge(gt_act, NT)
            pe.wait_ge(g_act, NT)
            pe.wait_ge(g_dve, NT)
            for c in range(C):
                for i in range(TC):
                    mm = pe.transpose(PS[0:2 * E1, c, i * P:(i + 1) * P], hot_w[:, c * TC + i, :], ident)
                mm.then_inc(hot_mm, 1)
            pe.wait_ge(yt_dve, NT)
            pe.wait_ge(xt_act, NT)
            for c in range(C):
                pe.wait_ge(hot_act, c + 1)
                for i in range(TC):
                    at = slice((c * TC + i) * P, (c * TC + i + 1) * P)
                    mm = pe.matmul(PS[:, C + c, i * P:(i + 1) * P], hot_wT[:, at], gains_sb[:, 2 * P:3 * P],
                                   start=True, stop=True)
                mm.then_inc(shift_mm, 1)
            for t in range(T):
                if t == T // 2:
                    pe.wait_ge(shift_act, C)
                pe.matmul(PS[:, t // 2, t % 2 * 2 * P:(t % 2 + 1) * 2 * P], hot_wT[:, t * P:(t + 1) * P],
                          gains_sb[:, 0:2 * P], start=True, stop=True).then_inc(gain_mm, 1)


_OUTS = [((N, P), "float32")]


def kernel(**inputs):
    import ml_dtypes
    import numpy as np
    import concourse.bacc as bacc
    from concourse.bass_utils import run_bass_kernel_spmd as run

    g = {k: np.asarray(v) for k, v in inputs.items()}

    def tiles(w):
        *lead, k, n = w.shape
        w = w.reshape(*lead, k // P, P, n)
        return np.ascontiguousarray(np.swapaxes(w, -3, -2)).reshape(*lead, P, k // P * n)

    mats = {"gru": g["L0_attn_W"].T, "conv": g["L0_ffn_conv_w"].transpose(1, 2, 0).reshape(P, 3 * P),
            "qkv": g["L0_ffn_wqkv"].T, "ident": np.eye(P, dtype=np.float32), "wo": g["L0_ffn_wo"].T,
            "gate": g["L0_ffn_gate_w"], "wr": g["L1_ffn_Wr"], "win": g["L1_attn_W_in"].T,
            "wdt": tiles(g["L1_attn_W_dt"].T), "wout": tiles(g["L1_attn_W_out"].T)}
    bqkv = g["L0_ffn_bqkv"].reshape(3, P)
    cols = {"conv_b": g["L0_ffn_conv_b"][:, None], "bq": bqkv[0][:, None], "bk": bqkv[1][:, None],
            "b1": g["L0_ffn_b1"].reshape(E0 * FT, P).T, "b_dt": g["L1_attn_b_dt"].reshape(2, P).T,
            "w_norm": g["L1_attn_w_norm"][:, None], "ln1_g": g["L0_ffn_ln1_g"][:, None],
            "ln1_b": g["L0_ffn_ln1_b"][:, None],
            "token": np.arange(N, dtype=np.float32).reshape(T, P).T,
            "spare": (2 * N + np.arange(NT * P, dtype=np.float32)).reshape(NT, P).T}
    rows = {"bv": bqkv[2], "bo": g["L0_ffn_bo"],
            "ln2_g": g["L0_ffn_ln2_g"], "ln2_b": g["L0_ffn_ln2_b"], "gate_b": g["L0_ffn_gate_b"],
            "br": g["L1_ffn_br"], "iota": np.arange(NT, dtype=np.float32)}
    gamma, beta = g["L1_ffn_gamma"], g["L1_ffn_beta"]
    gains = np.zeros((2, E1, 3, P), np.float32)
    gains[0, :, 0], gains[1, :, 1], gains[0, :, 2], gains[1, :, 2] = gamma, gamma, beta, beta
    w_all = np.concatenate([g["L1_ffn_W1"], g["L1_ffn_W3"], tiles(g["L1_ffn_W2"])], axis=2)
    pick = np.zeros((PARTS, PICK, E0, P), np.uint16)
    for e in range(E0):
        pick[:, e, e] = 0x3F80
    arrays = {
        "x": g["L0_attn_x"].reshape(N, P),
        "mats": np.concatenate([mats[k] for k in MATS], axis=1),
        "cols": np.concatenate([cols[k] for k in COLS], axis=1),
        "rows": np.concatenate([rows[k] for k in ROWS]),
        "b2": g["L0_ffn_b2"], "gains": gains.reshape(2 * E1, 3 * P), "pick": pick.reshape(PARTS * PICK, E0 * P).view(ml_dtypes.bfloat16),
        "w1": g["L0_ffn_w1"], "w2": tiles(g["L0_ffn_w2"]),
        "tri": np.concatenate([np.triu(np.ones((P, P), ml_dtypes.bfloat16), 1),
                               np.ones((P, P), ml_dtypes.bfloat16)], axis=1),
        "w_all": w_all.transpose(1, 0, 2).reshape(P, E1 * W_ALL),
    }
    nc = bacc.Bacc("TRN2", target_bir_lowering=False, num_devices=1)
    feeds, args = {}, {}
    for name, a in arrays.items():
        a = np.ascontiguousarray(a)
        feeds[f"in_{name}"] = a
        args[name] = nc.dram_tensor(f"in_{name}", a.shape, mybir.dt.from_np(a.dtype), kind="ExternalInput").ap()
    args["out"] = nc.dram_tensor("out_0", [N, P], F32, kind="ExternalOutput").ap()
    build(nc, **args)
    r = run(nc, [feeds], core_ids=[0])
    return r.results[0]["out_0"].reshape(1, N, P)
```
